# Optimizing a Trainium2 kernel written in Bass

```python
import numpy as np
import jax
import jax.numpy as jnp

def _softmax(x, axis=-1):
    return jax.nn.softmax(x, axis=axis)

def _gelu(x):
    return jax.nn.gelu(x, approximate=True)

def _silu(x):
    return jax.nn.silu(x)

def _sigmoid(x):
    return jax.nn.sigmoid(x)

def _layernorm(x, axis=-1, eps=1e-05):
    m = jnp.mean(x, axis=axis, keepdims=True)
    v = jnp.var(x, axis=axis, keepdims=True)
    return (x - m) / jnp.sqrt(v + eps)

def _scatter_add(tgt, idx, src, axis=0):
    return tgt.at[idx].add(src)

def _segment_sum(src, seg, n):
    return jax.ops.segment_sum(src, seg, n)
kernel_name = 'mk_prb_d1_jaxref_r8_897815'

def setup_inputs(seed: int=0):
    np.random.seed(seed)
    _w = jnp.asarray

    def _L0_attn_setup():
        import jax, jax.numpy as jnp
        import numpy as np
        H = 16
        DK = 128
        DV = 128
        M = 64
        EPS = 1e-05
        CLAMP = 32.0
        ROPE_BASE = 10000.0

        def _rope(x, cos, sin):
            x1, x2 = jnp.split(x, 2, axis=-1)
            return jnp.concatenate([x1 * cos - x2 * sin, x2 * cos + x1 * sin], axis=-1)
        key = jax.random.key(seed)
        ks = jax.random.split(key, 9)
        B, T, D = (1, 256, 256)
        sc = 0.02
        return {'hidden_states': jax.random.normal(ks[0], (B, T, D), jnp.float32), 'Wq': jax.random.normal(ks[1], (H * DK, D), jnp.float32) * sc, 'Wk': jax.random.normal(ks[2], (H * DK, D), jnp.float32) * sc, 'Wv': jax.random.normal(ks[3], (H * DV, D), jnp.float32) * sc, 'Wg': jax.random.normal(ks[4], (H * DV, D), jnp.float32) * sc, 'Wo': jax.random.normal(ks[5], (D, H * DV), jnp.float32) * sc, 'Ws1': jax.random.normal(ks[6], (16, D), jnp.float32) * sc, 'Ws2': jax.random.normal(ks[7], (H * M, 16), jnp.float32) * sc, 'bs2': jnp.zeros((H * M,), jnp.float32), 'g_norm_weight': jnp.ones((DV,), jnp.float32)}
    _L0_attn_in = _L0_attn_setup()

    def _L0_ffn_setup():
        import jax, jax.numpy as jnp
        import numpy as np
        BLOCK_SIZE = 32
        HIDDEN_SIZE = 256
        MLP_DIM = 2048
        NVFP4_LUT = jnp.array([0.0, 0.5, 1.0, 1.5, 2.0, 3.0, 4.0, 6.0, 0.0, -0.5, -1.0, -1.5, -2.0, -3.0, -4.0, -6.0], dtype=jnp.float32)

        def dequant_nvfp4(W_packed, scales, block=BLOCK_SIZE):
            N = W_packed.shape[0]
            low = W_packed & 15
            high = W_packed >> 4 & 15
            idx = jnp.stack([low, high], axis=-1).reshape(N, -1)
            vals = NVFP4_LUT[idx]
            K = vals.shape[1]
            vals = vals.reshape(N, K // block, block) * scales[:, :, None]
            return vals.reshape(N, K)
        key = jax.random.key(seed)
        ks = jax.random.split(key, 7)
        x = jax.random.normal(ks[0], (4, 32, HIDDEN_SIZE), dtype=jnp.float32)
        gate_W_packed = jax.random.randint(ks[1], (MLP_DIM, HIDDEN_SIZE // 2), 0, 32, dtype=jnp.int32)
        gate_scales = jax.random.uniform(ks[2], (MLP_DIM, HIDDEN_SIZE // BLOCK_SIZE), dtype=jnp.float32) * 0.1 + 0.001
        up_W_packed = jax.random.randint(ks[3], (MLP_DIM, HIDDEN_SIZE // 2), 0, 32, dtype=jnp.int32)
        up_scales = jax.random.uniform(ks[4], (MLP_DIM, HIDDEN_SIZE // BLOCK_SIZE), dtype=jnp.float32) * 0.1 + 0.001
        down_W_packed = jax.random.randint(ks[5], (HIDDEN_SIZE, MLP_DIM // 2), 0, 32, dtype=jnp.int32)
        down_scales = jax.random.uniform(ks[6], (HIDDEN_SIZE, MLP_DIM // BLOCK_SIZE), dtype=jnp.float32) * 0.1 + 0.001
        return {'x': x, 'gate_W_packed': gate_W_packed, 'gate_scales': gate_scales, 'up_W_packed': up_W_packed, 'up_scales': up_scales, 'down_W_packed': down_W_packed, 'down_scales': down_scales}
    _L0_ffn_in = _L0_ffn_setup()
    _d = {'L0_attn_hidden_states': _L0_attn_in['hidden_states'], 'L0_attn_Wq': _L0_attn_in['Wq'], 'L0_attn_Wk': _L0_attn_in['Wk'], 'L0_attn_Wv': _L0_attn_in['Wv'], 'L0_attn_Wg': _L0_attn_in['Wg'], 'L0_attn_Wo': _L0_attn_in['Wo'], 'L0_attn_Ws1': _L0_attn_in['Ws1'], 'L0_attn_Ws2': _L0_attn_in['Ws2'], 'L0_attn_bs2': _L0_attn_in['bs2'], 'L0_attn_g_norm_weight': _L0_attn_in['g_norm_weight'], 'L0_ffn_gate_W_packed': _L0_ffn_in['gate_W_packed'], 'L0_ffn_gate_scales': _L0_ffn_in['gate_scales'], 'L0_ffn_up_W_packed': _L0_ffn_in['up_W_packed'], 'L0_ffn_up_scales': _L0_ffn_in['up_scales'], 'L0_ffn_down_W_packed': _L0_ffn_in['down_W_packed'], 'L0_ffn_down_scales': _L0_ffn_in['down_scales']}
    _x0 = _d['L0_attn_hidden_states']
    _d['L0_attn_hidden_states'] = jax.random.normal(jax.random.fold_in(jax.random.key(seed), 1), (8, 256, 256), dtype=_x0.dtype)
    del _x0
    return _d

def reference(L0_attn_hidden_states, L0_attn_Wq, L0_attn_Wk, L0_attn_Wv, L0_attn_Wg, L0_attn_Wo, L0_attn_Ws1, L0_attn_Ws2, L0_attn_bs2, L0_attn_g_norm_weight, L0_ffn_gate_W_packed, L0_ffn_gate_scales, L0_ffn_up_W_packed, L0_ffn_up_scales, L0_ffn_down_W_packed, L0_ffn_down_scales):

    def _L0_attn_ref(hidden_states, Wq, Wk, Wv, Wg, Wo, Ws1, Ws2, bs2, g_norm_weight):
        import jax, jax.numpy as jnp
        import numpy as np
        H = 16
        DK = 128
        DV = 128
        M = 64
        EPS = 1e-05
        CLAMP = 32.0
        ROPE_BASE = 10000.0

        def _rope(x, cos, sin):
            x1, x2 = jnp.split(x, 2, axis=-1)
            return jnp.concatenate([x1 * cos - x2 * sin, x2 * cos + x1 * sin], axis=-1)
        B, T, D = hidden_states.shape
        hs = hidden_states
        q = (hs @ Wq.T).reshape(B, T, H, DK)
        k = (hs @ Wk.T).reshape(B, T, H, DK)
        pos = jnp.arange(T, dtype=jnp.float32)
        inv_freq = 1.0 / ROPE_BASE ** (jnp.arange(0, DK, 2, dtype=jnp.float32) / DK)
        ang = pos[:, None] * inv_freq[None, :]
        cos = jnp.cos(ang)[None, :, None, :]
        sin = jnp.sin(ang)[None, :, None, :]
        q = _rope(q, cos, sin).transpose(0, 2, 1, 3)
        k = _rope(k, cos, sin).transpose(0, 2, 1, 3)
        v = (hs @ Wv.T).reshape(B, T, H, DV).transpose(0, 2, 1, 3)
        s = hs @ Ws1.T @ Ws2.T + bs2
        s = jnp.clip(s, -CLAMP, CLAMP).reshape(B, T, H, M).transpose(0, 2, 1, 3)
        z = jax.lax.cumlogsumexp(s, axis=2)
        es = jnp.exp(s)
        enz = jnp.exp(-z)
        scale = DK ** (-0.5)
        mask = jnp.tril(jnp.ones((T, T), dtype=bool))
        A = jnp.einsum('bhtd,bhjd->bhtj', q, k) * scale
        A = jnp.where(mask, A, 0.0)
        ok = enz * jnp.einsum('bhtj,bhjm->bhtm', A, es)
        qv = jax.nn.softmax(ok, axis=-1)
        W2 = jnp.einsum('bhtm,bhjm->bhtj', qv * enz, es)
        W2 = jnp.where(mask, W2, 0.0)
        o = jnp.einsum('bhtj,bhjd->bhtd', W2, v)
        o = o.transpose(0, 2, 1, 3)
        g = (hs @ Wg.T).reshape(B, T, H, DV)
        o_n = o * jax.lax.rsqrt(jnp.mean(o * o, axis=-1, keepdims=True) + EPS) * g_norm_weight
        o_g = o_n * (g * jax.nn.sigmoid(g))
        return o_g.reshape(B, T, H * DV) @ Wo.T

    def _L0_ffn_ref(x, gate_W_packed, gate_scales, up_W_packed, up_scales, down_W_packed, down_scales):
        import jax, jax.numpy as jnp
        import numpy as np
        BLOCK_SIZE = 32
        HIDDEN_SIZE = 256
        MLP_DIM = 2048
        NVFP4_LUT = jnp.array([0.0, 0.5, 1.0, 1.5, 2.0, 3.0, 4.0, 6.0, 0.0, -0.5, -1.0, -1.5, -2.0, -3.0, -4.0, -6.0], dtype=jnp.float32)

        def dequant_nvfp4(W_packed, scales, block=BLOCK_SIZE):
            N = W_packed.shape[0]
            low = W_packed & 15
            high = W_packed >> 4 & 15
            idx = jnp.stack([low, high], axis=-1).reshape(N, -1)
            vals = NVFP4_LUT[idx]
            K = vals.shape[1]
            vals = vals.reshape(N, K // block, block) * scales[:, :, None]
            return vals.reshape(N, K)
        B, S, H = x.shape
        xt = x.reshape(B * S, H)
        Wg = dequant_nvfp4(gate_W_packed, gate_scales)
        Wu = dequant_nvfp4(up_W_packed, up_scales)
        Wd = dequant_nvfp4(down_W_packed, down_scales)
        gate = jnp.einsum('th,nh->tn', xt, Wg)
        up = jnp.einsum('th,nh->tn', xt, Wu)
        gelu = jnp.tanh(0.7978845608028654 * (gate + 0.044715 * gate ** 3)) * gate * 0.5 + gate * 0.5
        inter = gelu * up
        out = jnp.einsum('tn,hn->th', inter, Wd)
        return out.reshape(B, S, H)
    x = L0_attn_hidden_states
    xn = _layernorm(x, axis=-1)
    x = x + _L0_attn_ref(xn, L0_attn_Wq, L0_attn_Wk, L0_attn_Wv, L0_attn_Wg, L0_attn_Wo, L0_attn_Ws1, L0_attn_Ws2, L0_attn_bs2, L0_attn_g_norm_weight) + _L0_ffn_ref(xn, L0_ffn_gate_W_packed, L0_ffn_gate_scales, L0_ffn_up_W_packed, L0_ffn_up_scales, L0_ffn_down_W_packed, L0_ffn_down_scales)
    return x

_drawn_inputs = setup_inputs


def setup_inputs(seed=0):
    import zlib

    import numpy as np

    out = dict(_drawn_inputs(seed))
    spreads = {'L0_attn_bs2': (0.0, 0.8), 'L0_attn_g_norm_weight': (1.0, 0.6)}
    factors = {'L0_attn_Wq': 8.0,
     'L0_attn_Wk': 8.0,
     'L0_attn_Wv': 5.463,
     'L0_attn_Wg': 5.522,
     'L0_attn_Wo': 5.464,
     'L0_attn_Ws1': 8.0,
     'L0_attn_Ws2': 8.0}
    for name, (base, spread) in spreads.items():
        noise = np.random.default_rng([zlib.crc32(name.encode()), seed]).standard_normal(out[name].shape)
        drawn = base * np.exp(spread * noise) if base else spread * noise
        out[name] = jnp.asarray(drawn.astype(out[name].dtype))
    for name, factor in factors.items():
        out[name] = (out[name] * factor).astype(out[name].dtype)
    return out
```

```python
from contextlib import ExitStack

import numpy as np

import concourse.bass as bass
from concourse import mybir

F32 = mybir.dt.float32
F32R = mybir.dt.float32r
F16 = mybir.dt.float16
I32 = mybir.dt.int32
ALU = mybir.AluOpType
ACT = mybir.ActivationFunctionType
AX_X = mybir.AxisListType.X

P = 128
B, T, D = 8, 256, 256
H, DK, DV, M = 16, 128, 128, 64
RANK = 16
MLP = 2048
HP = H // 2
BP = B // 2
TOK = 2 * T
KT = D // P
NT = TOK // P
NF = MLP // HP
EPS = 1e-5
CLAMP = 32.0
SCALE = DK ** -0.5
GELU_A, GELU_C = 0.044715, 0.7978845608028654
STEPS = HP * BP
W_VG, W_QK, W_GU, W_OD = range(4)
SC_SLOTS = {"A": (0, 1, 2, 3), "S": (4,), "W": (5, 6, 9, 10), "E": (7, 8)}
SC_STEP = 11


def build(nc, x, w_qkvg, w_packed, w_scaled, w_slot, w_slot1, g_norm, rope_tab, out):
    with ExitStack() as ctx:
        def sb(name, shape, dt=F32):
            return ctx.enter_context(nc.sbuf_tensor(name, shape, dt))

        def sem(name):
            return ctx.enter_context(nc.semaphore(name))

        acc = sb("acc", [P, BP * NT, D])
        xh = sb("xh", [P, KT, B * T], F32R)
        xl = sb("xl", [P, KT, B * T], F32R)
        wqk = [sb(f"wqk_{s}", [P, KT, 512], F32R) for s in ("hi", "lo")]
        wvg = [sb(f"wvg_{s}", [P, KT, 512], F32R) for s in ("hi", "lo")]
        wgu = [sb(f"wgu_{s}", [P, KT, 512], F32R) for s in ("hi", "lo")]
        wod = [sb(f"wod_{s}", [P, 4, D], F32R) for s in ("hi", "lo")]
        raw = sb("raw", [P, KT * 1024])
        packed = sb("packed", [P, 768], I32)
        codes = sb("codes", [P, 768], I32)
        scaled = sb("scaled", [P, 1280])
        ws2 = sb("ws2", [P, P])
        h1 = sb("h1", [P, TOK])
        gn = sb("gn", [P, 1])
        rope = sb("rope", [P, 2, T])
        mask_a = sb("mask_a", [P, 2, P])
        mask_w = sb("mask_w", [P, 2, P])
        ident = sb("ident", [P, P])
        esT = [sb(f"esT{i}", [P, TOK]) for i in range(2)]
        enzT = [sb(f"enzT{i}", [P, TOK]) for i in range(2)]
        esJ = sb("esJ", [P, NT, P])
        enzJ = sb("enzJ", [P, TOK])
        qkT = sb("qkT", [P, 4, TOK])
        xs = [sb(f"xs{i}", [P, TOK]) for i in range(2)]
        ra = [sb(f"ra{i}", [P, TOK]) for i in range(2)]
        vS = [sb(f"vS{i}", [P, NT, 256]) for i in range(2)]
        G = [sb(f"G{i}", [P, NT * 256]) for i in range(2)]
        th = [sb(f"th{i}", [P, 256]) for i in range(2)]
        At = [sb(f"At{i}", [P, 3, P]) for i in range(4)]
        Wt = [sb(f"Wt{i}", [P, 3, P]) for i in range(4)]
        sm = sb("sm", [P, TOK])
        qe = sb("qe", [P, TOK])
        osq = sb("osq", [P, TOK])
        og = sb("og", [P, NT * 256])
        ogT = [[sb(f"ogT_{s}{h}", [P, TOK], F32R) for h in range(2)] for s in ("hi", "lo")]
        inter = [[sb(f"inter_{s}{e}", [P, TOK], F32R) for e in range(2)] for s in ("hi", "lo")]
        ffa = [sb(f"ffa{i}", [P, TOK]) for i in range(2)]
        ffb = [sb(f"ffb{i}", [P, TOK]) for i in range(2)]
        mx = sb("mx", [P, 8])
        ssum = sb("ssum", [P, 8])
        rs = sb("rs", [P, 8])
        rs2 = sb("rs2", [P, 8])
        ms = sb("ms", [P, 8])
        msn = sb("msn", [P, 8])
        mse = sb("mse", [P, 8])
        rstd = sb("rstd", [P, 8])
        scal = sb("scal", [P, 8])
        mhalf = sb("mhalf", [P, 8])
        bns = sb("bns", [P, NT, 6])
        mv = sb("mv", [P, NT, 2])

        bank = [ctx.enter_context(nc.psum_tensor(f"bank{i}", [P, 512], F32)) for i in range(8)]
        pj = bank[0:4]
        sc = bank[4:6]
        rg = bank[6:8]

        x_in = [sem(f"x_in{i}") for i in range(BP)]
        raw_in, packed_in, scaled_in, ws2_in = sem("raw_in"), sem("packed_in"), sem("scaled_in"), sem("ws2_in")
        ws1_in, const_in, out_sent = sem("ws1_in"), sem("const_in"), sem("out_sent")
        A_full, S_full, W_full, E_full = sem("A_full"), sem("S_full"), sem("W_full"), sem("E_full")
        ok_full, pT_full, o_full, ogT_full, out_full = (
            sem("ok_full"), sem("pT_full"), sem("o_full"), sem("ogT_full"), sem("out_full"))
        vg_full, qk_full, ffn_full = sem("vg_full"), sem("qk_full"), sem("ffn_full")
        xT_full, h1_full = sem("xT_full"), sem("h1_full")
        A_off, W_off, v_ready, gtanh, p_ready, osq_done = (
            sem("A_off"), sem("W_off"), sem("v_ready"), sem("gtanh"), sem("p_ready"), sem("osq_done"))
        ogT_hi, ff_sq, ff_tanh, inter_hi = sem("ogT_hi"), sem("ff_sq"), sem("ff_tanh"), sem("inter_hi")
        swapped, es_ready, J_ready, w_hi = sem("swapped"), sem("es_ready"), sem("J_ready"), sem("w_hi")
        xh_done, h1_done, ws1_hi = sem("xh_done"), sem("h1_done"), sem("ws1_hi")
        A_diag, W_diag, G_ready, okz_done, mx_done = (
            sem("A_diag"), sem("W_diag"), sem("G_ready"), sem("okz_done"), sem("mx_done"))
        ssum_done, rs_done, rs2_done, ms_done, msn_done, mse_done, scal_done = (
            sem("ssum_done"), sem("rs_done"), sem("rs2_done"), sem("ms_done"), sem("msn_done"),
            sem("mse_done"), sem("scal_done"))
        og_done, ogT_lo, acc_done, qe_ready = sem("og_done"), sem("ogT_lo"), sem("acc_done"), sem("qe_ready")
        ff_poly, ff_arg, ff_gelu, inter_done = sem("ff_poly"), sem("ff_arg"), sem("ff_gelu"), sem("inter_done")
        cos_done, sin_done, clip_done, scan_done, enz_ready = (
            sem("cos_done"), sem("sin_done"), sem("clip_done"), sem("scan_done"), sem("enz_ready"))
        code_step, mlp_w, out_w = sem("code_step"), sem("mlp_w"), sem("out_w")
        bn_done, mv_done, var_done, xn_done, xl_done = (
            sem("bn_done"), sem("mv_done"), sem("var_done"), sem("xn_done"), sem("xl_done"))
        roped, sub_done, inter_lo, pow_done, w_lo = (
            sem("roped"), sem("sub_done"), sem("inter_lo"), sem("pow_done"), sem("w_lo"))
        const_set, consts, ws1_lo, xpow_done = sem("const_set"), sem("consts"), sem("ws1_lo"), sem("xpow_done")

        x_rows = x.rearrange("b (n p) d -> p (b n) d", p=P)
        out_rows = out.rearrange("b (n p) d -> p (b n) d", p=P)
        raw_k = raw[:, :].rearrange("p (k n) -> p k n", k=KT)
        mlp_raw = raw[:, 0:1024].rearrange("p (k n) -> p k n", k=KT)
        od_raw = raw[:, 1024:2048]
        xn = og[:, :].rearrange("p (n d) -> p n d", n=NT)
        ws1 = osq[:, 0:KT * P].rearrange("p (k n) -> p k n", k=KT)
        ws1_s = [ogT[s][0][:, 0:KT * P].rearrange("p (k n) -> p k n", k=KT) for s in range(2)]
        xhl = (xh, xl)

        def wait(eng, s, value):
            if not isinstance(value, int) or value > 0:
                eng.wait_ge(s, value)

        def tokens(bp, tile=None):
            return slice(bp * TOK, (bp + 1) * TOK) if tile is None else slice(
                bp * TOK + tile * P, bp * TOK + (tile + 1) * P)

        def sc_bank(bp, kind, i=0):
            return sc[(SC_STEP * bp + SC_SLOTS[kind][i]) % 2]

        def each_stage(eng, stage):
            for bp in range(BP):
                stage(0, bp, bp == 0, False)
            with eng.Fori(1, HP - 1) as hp:
                for bp in range(BP):
                    stage(hp, bp, False, False)
            for bp in range(BP):
                stage(HP - 1, bp, False, bp == BP - 1)

        def three(pe, dst, stat, mov, start, stop):
            pe.matmul(dst, stat[0], mov[0], start=start, stop=False)
            pe.matmul(dst, stat[0], mov[1], start=False, stop=False)
            return pe.matmul(dst, stat[1], mov[0], start=False, stop=stop)

        block = ctx.enter_context(nc.Block())

        @block.sync
        def _(sp):
            def load_ws2(hp):
                for g in range(BP):
                    sp.dma_start(ws2[32 * g:32 * g + RANK + 1, :], w_slot[hp]).then_inc(ws2_in, 16)

            for bp in range(BP):
                sp.dma_start(acc[:, bp * NT:(bp + 1) * NT, :],
                             x_rows[:, bp * NT:(bp + 1) * NT, :]).then_inc(x_in[bp], 16)
                if bp == 0:
                    sp.dma_start(ws1, w_slot1).then_inc(ws1_in, 16)
                    sp.dma_start(raw[:, :], w_qkvg[0]).then_inc(raw_in, 16)
                    load_ws2(0)
                    sp.dma_start(rope[:, :, :], rope_tab).then_inc(const_in, 16)
                    sp.dma_start(gn[:, :], g_norm).then_inc(const_in, 16)
                if bp == 1:
                    sp.dma_start(packed[:, :], w_packed[0]).then_inc(packed_in, 16)
                    sp.dma_start(scaled[:, :], w_scaled[0]).then_inc(scaled_in, 16)
            with sp.Fori(0, HP - 1) as hp:
                sp.wait_ge(w_lo, 4 * hp + 4)
                sp.dma_start(raw[:, :], w_qkvg[hp + 1]).then_inc(raw_in, 16)
                sp.dma_start(packed[:, :], w_packed[hp + 1]).then_inc(packed_in, 16)
                sp.dma_start(scaled[:, :], w_scaled[hp + 1]).then_inc(scaled_in, 16)
                sp.wait_ge(S_full, BP * (hp + 1))
                load_ws2(hp + 1)
            for bp in range(BP):
                sp.wait_ge(acc_done, 2 * ((HP - 1) * BP + bp + 1))
                sp.dma_start(out_rows[:, bp * NT:(bp + 1) * NT, :],
                             acc[:, bp * NT:(bp + 1) * NT, :]).then_inc(out_sent, 16)
            sp.wait_ge(out_sent, 16 * BP)

        @block.tensor
        def _(pe):
            def project_vg(n, bp, hp, i, free):
                if i == 0:
                    wait(pe, w_lo, 4 * hp + W_VG + 1)
                if free:
                    pe.wait_ge(cos_done, 4 * (n - 1) + i + 1)
                for k in range(KT):
                    mm = three(pe, pj[i][:, :], [a[:, k, tokens(bp, i)] for a in xhl],
                               [w[:, k, :] for w in wvg], k == 0, k == KT - 1)
                mm.then_inc(vg_full, 1)

            def project_qk(n, bp, hp, i, st):
                if i == 0:
                    wait(pe, w_lo, 4 * hp + W_QK + 1)
                if st is None:
                    pe.wait_ge(G_ready, i + 1)
                else:
                    pe.wait_ge(ff_gelu if i % 2 == 0 else inter_done, 2 * st + i // 2 + 1)
                for k in range(KT):
                    mm = three(pe, pj[i][:, :], [w[:, k, i * P:(i + 1) * P] for w in wqk],
                               [a[:, k, tokens(bp)] for a in xhl], k == 0, k == KT - 1)
                mm.then_inc(qk_full, 1)

            def mlp_up(st, bp, hp, i, last):
                if i == 0:
                    wait(pe, w_lo, 4 * hp + W_GU + 1)
                if last:
                    pe.wait_ge(cos_done, 4 * st + i + 1)
                else:
                    pe.wait_ge(G_ready, 4 * (st + 1) + i + 1)
                col = (i % 2 * 2 + i // 2) * P
                for k in range(KT):
                    mm = three(pe, pj[i][:, :], [w[:, k, col:col + P] for w in wgu],
                               [a[:, k, tokens(bp)] for a in xhl], k == 0, k == KT - 1)
                mm.then_inc(ffn_full, 1)

            def slot_scores(n, bp, hp):
                if bp == 0:
                    wait(pe, ws2_in, 16 * BP * (hp + 1))
                g = slice(32 * bp, 32 * bp + RANK + 1)
                pe.matmul(sc_bank((bp - 1) % BP, "S")[:, :] if n is not None else sc[1][:, :],
                          ws2[g, :], h1[g, :], start=True, stop=True).then_inc(S_full, 1)

            def slot_transpose(dst, src):
                for i in range(NT):
                    mm = pe.transpose(dst[:, i * P:(i + 1) * P], src[:, i * P:(i + 1) * P], ident[:, :])
                mm.then_inc(E_full, 1)

            def scores(st, bp, i, hp):
                h, b = i // 2, i % 2
                if b == 0:
                    pe.wait_ge(roped, 4 * st + 2 * h + 2)
                dst = sc_bank(bp, "A", i)
                t0 = b * T
                pe.matmul(dst[:, 0:T], qkT[:, 2 * h + 1, t0:t0 + P], qkT[:, 2 * h, t0:t0 + T],
                          start=True, stop=True)
                pe.matmul(dst[:, T:T + P], qkT[:, 2 * h + 1, t0 + P:t0 + T], qkT[:, 2 * h, t0 + P:t0 + T],
                          start=True, stop=True).then_inc(A_full, 1)

            def slot_reads(st):
                pe.wait_ge(A_off, 4 * st + 4)
                pe.wait_ge(J_ready, 2 * st + 1)
                for b in range(2):
                    for h in range(2):
                        a = At[2 * h + b]
                        c = b * 256 + h * M
                        pe.matmul(rg[0][:, c:c + M], a[:, 0, :], esJ[:, 2 * b, h * M:(h + 1) * M],
                                  start=True, stop=True)
                        c += P
                        pe.matmul(rg[0][:, c:c + M], a[:, 1, :], esJ[:, 2 * b, h * M:(h + 1) * M],
                                  start=True, stop=False)
                        mm = pe.matmul(rg[0][:, c:c + M], a[:, 2, :], esJ[:, 2 * b + 1, h * M:(h + 1) * M],
                                       start=False, stop=True)
                mm.then_inc(ok_full, 1)

            def slot_weights(st, bp, i):
                h, b = i // 2, i % 2
                dst = sc_bank(bp, "W", i)
                g = slice(h * M, (h + 1) * M)
                t0 = b * T
                pe.matmul(dst[:, 0:T], esT[bp % 2][g, t0:t0 + P], qe[g, t0:t0 + T], start=True, stop=True)
                pe.matmul(dst[:, T:T + P], esT[bp % 2][g, t0 + P:t0 + T], qe[g, t0 + P:t0 + T],
                          start=True, stop=True).then_inc(W_full, 1)

            def values(st, bp, b):
                for h in range(2):
                    w = Wt[2 * h + b]
                    v0 = vS[bp % 2][:, 2 * b, h * DV:(h + 1) * DV]
                    v1 = vS[bp % 2][:, 2 * b + 1, h * DV:(h + 1) * DV]
                    c = h * DV
                    pe.matmul(rg[b][:, c:c + DV], w[:, 0, :], v0, start=True, stop=True)
                    c += 256
                    pe.matmul(rg[b][:, c:c + DV], w[:, 1, :], v0, start=True, stop=False)
                    mm = pe.matmul(rg[b][:, c:c + DV], w[:, 2, :], v1, start=False, stop=True)
                mm.then_inc(o_full, 1)

            def gated_transpose(done):
                pe.wait_ge(og_done, 2 * done)
                for h in range(2):
                    for i in range(NT):
                        mm = pe.transpose(rg[h][:, i * P:(i + 1) * P],
                                          og[:, i * 256 + h * DV:i * 256 + (h + 1) * DV], ident[:, :])
                    mm.then_inc(ogT_full, 1)

            def outputs(done, b, hp, free_okz):
                if b == 0:
                    pe.wait_ge(ogT_hi, 2 * done)
                    pe.wait_ge(ogT_lo, 2 * done)
                    pe.wait_ge(inter_lo, 2 * done)
                    wait(pe, w_lo, 4 * hp + W_OD + 1)
                elif free_okz is not None:
                    pe.wait_ge(okz_done, free_okz)
                for tt in range(2):
                    cols = slice((2 * b + tt) * P, (2 * b + tt + 1) * P)
                    for s in range(4):
                        src = ogT if s < 2 else inter
                        mm = three(pe, rg[1 - b][:, tt * D:(tt + 1) * D],
                                   [src[u][s % 2][:, cols] for u in range(2)],
                                   [w[:, s, :] for w in wod], s == 0, s == 3)
                mm.then_inc(out_full, 1)

            def transpose_x(bp):
                pe.wait_ge(xn_done, bp + 1)
                for k in range(KT):
                    if bp:
                        pe.wait_ge(xh_done, KT * (bp - 1) + k + 1)
                        pe.wait_ge(xl_done, KT * (bp - 1) + k + 1)
                    for i in range(NT):
                        mm = pe.transpose(rg[k][:, i * P:(i + 1) * P], xn[:, i, k::KT], ident[:, :])
                    mm.then_inc(xT_full, 1)

            def slot_inner(bp, dst):
                pe.wait_ge(xl_done, KT * (bp + 1))
                pe.wait_ge(xh_done, KT * (bp + 1))
                for k in range(KT):
                    mm = three(pe, dst[:, :], [w[:, k, :] for w in ws1_s],
                               [a[:, k, tokens(bp)] for a in xhl], k == 0, k == KT - 1)
                mm.then_inc(h1_full, 1)

            pe.wait_ge(consts, 1)
            transpose_x(0)
            pe.wait_ge(ws1_lo, 1)
            slot_inner(0, sc[0])
            for i in range(NT):
                project_vg(0, 0, 0, i, False)
            pe.wait_ge(h1_done, 1)
            slot_scores(None, 0, 0)
            transpose_x(1)
            pe.wait_ge(es_ready, 1)
            slot_transpose(sc[0], esT[0])
            pe.wait_ge(enz_ready, 2)
            slot_transpose(sc[1], enzT[0])
            pe.wait_ge(J_ready, 1)
            slot_inner(1, sc[0])
            for i in range(4):
                project_qk(0, 0, 0, i, None)
            transpose_x(2)
            pe.wait_ge(J_ready, 2)
            slot_inner(2, sc[1])
            transpose_x(3)
            pe.wait_ge(h1_done, 2)
            slot_inner(3, sc[0])

            def stage(hp, bp, first, last):
                st = 4 * hp + bp
                nbp = (bp + 1) % BP
                nhp = hp + 1 if bp == BP - 1 else hp
                php = hp - 1 if bp == 0 else hp
                for i in (0, 1):
                    if first:
                        pe.wait_ge(h1_done, 4 - i)
                    else:
                        pe.wait_ge(W_off, 4 * (st - 1) + i + 3)
                    scores(st, bp, i, hp)
                if not last:
                    project_vg(st + 1, nbp, nhp, 0, True)
                pe.wait_ge(A_off, 4 * st + 1)
                scores(st, bp, 2, hp)
                if not last:
                    project_vg(st + 1, nbp, nhp, 1, True)
                pe.wait_ge(A_off, 4 * st + 2)
                scores(st, bp, 3, hp)
                if not last:
                    pe.wait_ge(A_off, 4 * st + 3)
                    slot_scores(st, nbp, nhp)
                if not first:
                    gated_transpose(st)
                if not last:
                    project_vg(st + 1, nbp, nhp, 2, True)
                    project_vg(st + 1, nbp, nhp, 3, True)
                if first:
                    pe.wait_ge(xl_done, KT * BP)
                    pe.wait_ge(xh_done, KT * BP)
                else:
                    pe.wait_ge(ogT_hi, 2 * st - 1)
                    pe.wait_ge(ogT_lo, 2 * st - 1)
                slot_reads(st)
                if not first:
                    outputs(st, 0, php, None)
                mlp_up(st, bp, hp, 0, last)
                if not first:
                    outputs(st, 1, php, st + 1)
                mlp_up(st, bp, hp, 1, last)
                pe.wait_ge(p_ready, st + 1)
                wait(pe, acc_done, 2 * st - 1)
                for i in range(NT):
                    mm = pe.transpose(rg[1][:, i * P:(i + 1) * P], sm[:, i * P:(i + 1) * P], ident[:, :])
                mm.then_inc(pT_full, 1)
                mlp_up(st, bp, hp, 2, last)
                pe.wait_ge(qe_ready, st + 1)
                pe.wait_ge(A_off, 4 * st + 4)
                slot_weights(st, bp, 0)
                mlp_up(st, bp, hp, 3, last)
                if not last:
                    pe.wait_ge(clip_done, st + 2)
                slot_weights(st, bp, 1)
                if not last:
                    pe.wait_ge(W_off, 4 * st + 1)
                    pe.wait_ge(es_ready, st + 2)
                    slot_transpose(sc_bank(bp, "E", 0), esT[nbp % 2])
                    pe.wait_ge(W_off, 4 * st + 2)
                    pe.wait_ge(enz_ready, 2 * (st + 2))
                    slot_transpose(sc_bank(bp, "E", 1), enzT[nbp % 2])
                    project_qk(st + 1, nbp, nhp, 0, st)
                    pe.wait_ge(J_ready, 2 * (st + 1) + 1)
                else:
                    pe.wait_ge(W_off, 4 * st + 1)
                slot_weights(st, bp, 2)
                if not last:
                    project_qk(st + 1, nbp, nhp, 1, st)
                    pe.wait_ge(J_ready, 2 * (st + 1) + 2)
                else:
                    pe.wait_ge(W_off, 4 * st + 2)
                slot_weights(st, bp, 3)
                if not last:
                    project_qk(st + 1, nbp, nhp, 2, st)
                pe.wait_ge(W_off, 4 * st + 3)
                pe.wait_ge(v_ready, 4 * st + 4)
                if first:
                    pe.wait_ge(okz_done, 1)
                else:
                    pe.wait_ge(acc_done, 2 * st)
                values(st, bp, 0)
                if not last:
                    project_qk(st + 1, nbp, nhp, 3, st)
                pe.wait_ge(W_off, 4 * st + 4)
                values(st, bp, 1)

            each_stage(pe, stage)
            gated_transpose(STEPS)
            outputs(STEPS, 0, HP - 1, None)
            outputs(STEPS, 1, HP - 1, None)

        @block.scalar
        def _(act):
            def split_hi(hp, which):
                if which == W_VG:
                    wait(act, vg_full, 16 * hp)
                    act.wait_ge(raw_in, 16 * hp + 16)
                    dst, src = wvg[0][:, :, :], raw_k[:, :, 512:1024]
                elif which == W_QK:
                    wait(act, qk_full, 16 * hp)
                    act.wait_ge(raw_in, 16 * hp + 16)
                    dst, src = wqk[0][:, :, :], raw_k[:, :, 0:512]
                elif which == W_GU:
                    wait(act, ffn_full, 16 * hp)
                    act.wait_ge(mlp_w, 2 * hp + 2)
                    dst, src = wgu[0][:, :, :], mlp_raw
                else:
                    wait(act, out_full, 8 * hp)
                    act.wait_ge(out_w, 3 * hp + 3)
                    dst, src = wod[0][:, :, :].rearrange("p s c -> p (s c)"), od_raw
                act.activation(dst, src, ACT.Copy).then_inc(w_hi, 1)

            def copy_v(n, par, i):
                act.wait_ge(vg_full, 4 * n + i + 1)
                if i == 0:
                    wait(act, o_full, 2 * (n - 1))
                act.activation(vS[par][:, i, :], pj[i][:, 0:256], ACT.Copy).then_inc(v_ready, 1)
                wait(act, G_ready, 4 * n + i - 1)
                act.activation(th[i % 2][:, :], pj[i][:, 256:512], ACT.Tanh, scale=0.5).then_inc(gtanh, 1)

            def swap_halves(n, i):
                act.wait_ge(qk_full, 4 * n + i + 1)
                wait(act, roped, 4 * n + i - 1)
                act.activation(xs[i % 2][0:64, :], pj[i][64:128, :], ACT.Copy)
                act.activation(xs[i % 2][64:128, :], pj[i][0:64, :], ACT.Copy).then_inc(swapped, 1)

            def slot_exp(n, par):
                act.wait_ge(clip_done, n + 1)
                act.activation(esT[par][:, :], esT[par][:, :], ACT.Exp).then_inc(es_ready, 1)

            def copy_J(n, which, src):
                act.wait_ge(E_full, 2 * n + which + 1)
                if which == 0:
                    wait(act, ok_full, n)
                    act.activation(esJ[:, :, :].rearrange("p n m -> p (n m)"), src, ACT.Copy).then_inc(J_ready, 1)
                else:
                    wait(act, okz_done, n)
                    act.activation(enzJ[:, :], src, ACT.Copy).then_inc(J_ready, 1)

            def off_diagonal(diag, done, dst, bp, kind, st, i, scale):
                act.wait_ge(diag, 4 * st + i + 1)
                act.activation(dst[i][:, 1, :], sc_bank(bp, kind, i)[:, P:2 * P], ACT.Copy,
                               scale=scale).then_inc(done, 1)

            def square_o(st, b):
                act.wait_ge(o_full, 2 * st + b + 1)
                wait(act, ms_done, 2 * st + b)
                act.activation(osq[:, :], rg[b][:, :], ACT.Square).then_inc(osq_done, 1)

            def gated_hi(done, h):
                act.wait_ge(ogT_full, 2 * (done - 1) + h + 1)
                wait(act, out_full, 2 * (done - 1))
                act.activation(ogT[0][h][:, :], rg[h][:, :], ACT.Copy).then_inc(ogT_hi, 1)

            def gate_square(st, e):
                act.wait_ge(ffn_full, 4 * st + 2 * e + 1)
                wait(act, inter_done, 2 * (st - 1) + e + 1)
                act.activation(ffa[e][:, :], pj[2 * e][:, :], ACT.Square).then_inc(ff_sq, 1)

            def gate_tanh(st, e):
                act.wait_ge(ff_arg, 2 * st + e + 1)
                act.activation(ffb[e][:, :], ffb[e][:, :], ACT.Tanh, scale=GELU_C).then_inc(ff_tanh, 1)

            def hidden_hi(st, e):
                act.wait_ge(inter_done, 2 * st + e + 1)
                wait(act, out_full, 2 * st)
                act.activation(inter[0][e][:, :], ffb[e][:, :], ACT.Copy).then_inc(inter_hi, 1)

            def x_hi(bp):
                for k in range(KT):
                    act.wait_ge(xT_full, KT * bp + k + 1)
                    act.activation(xh[:, k, tokens(bp)], rg[k][:, :], ACT.Copy).then_inc(xh_done, 1)

            def inner_copy(bp, src):
                act.wait_ge(h1_full, bp + 1)
                act.activation(h1[32 * bp:32 * bp + RANK, :], src[0:RANK, :], ACT.Copy).then_inc(h1_done, 1)

            act.wait_ge(ws1_in, 16)
            for k in range(KT):
                ins = act.activation(ws1_s[0][:, k, :], ws1[:, k, :], ACT.Copy)
            ins.then_inc(ws1_hi, 1)
            act.wait_ge(const_set, 4)
            split_hi(0, W_VG)
            x_hi(0)
            inner_copy(0, sc[0])
            split_hi(0, W_QK)
            for i in range(NT):
                copy_v(0, 0, i)
            slot_exp(0, 0)
            x_hi(1)
            copy_J(0, 0, sc[0][:, :])
            copy_J(0, 1, sc[1][:, :])
            inner_copy(1, sc[0])
            for i in range(4):
                swap_halves(0, i)
            x_hi(2)
            inner_copy(2, sc[1])
            x_hi(3)
            inner_copy(3, sc[0])
            split_hi(0, W_GU)

            def stage(hp, bp, first, last):
                st = 4 * hp + bp
                npar = (bp + 1) % 2
                a_args = (A_diag, A_off, At, bp, "A", st)
                w_args = (W_diag, W_off, Wt, bp, "W", st)
                off_diagonal(*a_args, 0, SCALE)
                off_diagonal(*a_args, 1, SCALE)
                if not last:
                    copy_v(st + 1, npar, 0)
                off_diagonal(*a_args, 2, SCALE)
                if not last:
                    copy_v(st + 1, npar, 1)
                off_diagonal(*a_args, 3, SCALE)
                if not first:
                    gated_hi(st, 0)
                    gated_hi(st, 1)
                if not last:
                    slot_exp(st + 1, npar)
                    copy_v(st + 1, npar, 2)
                    copy_v(st + 1, npar, 3)
                act.wait_ge(sub_done, st + 1)
                act.activation(sm[:, :], sm[:, :], ACT.Exp).then_inc(p_ready, 1)
                if first:
                    split_hi(0, W_OD)
                gate_square(st, 0)
                gate_tanh(st, 0)
                if bp == 2 and not (isinstance(hp, int) and hp == HP - 1):
                    split_hi(hp + 1, W_VG)
                off_diagonal(*w_args, 0, 1.0)
                hidden_hi(st, 0)
                gate_square(st, 1)
                off_diagonal(*w_args, 1, 1.0)
                gate_tanh(st, 1)
                if not last:
                    copy_J(st + 1, 0, sc_bank(bp, "E", 0)[:, :])
                    copy_J(st + 1, 1, sc_bank(bp, "E", 1)[:, :])
                hidden_hi(st, 1)
                if not last:
                    swap_halves(st + 1, 0)
                off_diagonal(*w_args, 2, 1.0)
                if not last:
                    swap_halves(st + 1, 1)
                off_diagonal(*w_args, 3, 1.0)
                if not last:
                    swap_halves(st + 1, 2)
                square_o(st, 0)
                if not last:
                    swap_halves(st + 1, 3)
                square_o(st, 1)
                more = not (isinstance(hp, int) and hp == HP - 1)
                if bp == 2 and more:
                    split_hi(hp + 1, W_QK)
                if bp == 3 and more:
                    split_hi(hp + 1, W_GU)
                if bp == 0 and not first:
                    split_hi(hp, W_OD)

            each_stage(act, stage)
            gated_hi(STEPS, 0)
            gated_hi(STEPS, 1)

        @block.vector
        def _(dve):
            cos = rope[:, 0, :].unsqueeze(1).to_broadcast([P, 2, T])
            sin = rope[:, 1, :].unsqueeze(1).to_broadcast([P, 2, T])

            def two(ap):
                return ap.rearrange("p (b t) -> p b t", b=2)

            def diagonal(full, done, dst, bp, kind, st, i, mask, used):
                dve.wait_ge(full, 4 * st + i + 1)
                wait(dve, *used)
                src = sc_bank(bp, kind, i)[:, 0:3 * P].rearrange("p (n t) -> p n t", n=3)
                dve.tensor_tensor(dst[i][:, 0:3:2, :], src[:, 0:3:2, :], mask[:, :, :], ALU.mult).then_inc(done, 1)

            def sum_squares(st, b):
                dve.wait_ge(osq_done, 2 * st + b + 1)
                wait(dve, msn_done, st)
                dve.tensor_reduce(ms[:, 4 * b:4 * b + 4], osq[:, :].rearrange("p (g d) -> p g d", g=4),
                                  AX_X, ALU.add).then_inc(ms_done, 1)

            def norm_arg(done):
                dve.wait_ge(ms_done, 2 * done)
                dve.wait_ge(rs2_done, done)
                wait(dve, mse_done, done - 1)
                dve.tensor_tensor(msn[:, :], ms[:, :], rs2[:, :], ALU.mult).then_inc(msn_done, 1)
                dve.wait_ge(msn_done, done)
                wait(dve, pow_done, done - 1)
                dve.tensor_scalar(mse[:, :], msn[:, :], 1.0 / DV, EPS, ALU.mult, ALU.add).then_inc(mse_done, 1)

            def gate_o(done, par):
                dve.wait_ge(pow_done, done)
                wait(dve, og_done, 2 * (done - 1))
                dve.tensor_tensor(scal[:, :], rstd[:, :], rs[:, :], ALU.mult).then_inc(scal_done, 1)
                dve.wait_ge(scal_done, done)
                wait(dve, ogT_full, 2 * (done - 1))
                for b in range(2):
                    for q in range(4):
                        c = slice((4 * b + q) * P, (4 * b + q + 1) * P)
                        ins = dve.scalar_tensor_tensor(
                            out=og[:, c], in0=rg[b][:, q * P:(q + 1) * P], scalar=scal[:, 4 * b + q:4 * b + q + 1],
                            in1=G[par][:, c], op0=ALU.mult, op1=ALU.mult)
                    ins.then_inc(og_done, 1)

            def gated_lo(done, h):
                dve.wait_ge(ogT_hi, 2 * (done - 1) + h + 1)
                wait(dve, out_full, 2 * (done - 1))
                dve.tensor_tensor(ogT[1][h][:, :], rg[h][:, :], ogT[0][h][:, :].bitcast(F32),
                                  ALU.subtract).then_inc(ogT_lo, 1)

            def clip(n, par, src):
                dve.wait_ge(S_full, n + 1)
                wait(dve, W_full, 4 * (n - 1))
                wait(dve, scan_done, 2 * (n - 1))
                dve.tensor_scalar(esT[par][:, :], src, CLAMP, -CLAMP, ALU.min, ALU.max).then_inc(clip_done, 1)

            def gate_g(n, par, i):
                dve.wait_ge(gtanh, 4 * n + i + 1)
                if i == 0:
                    wait(dve, og_done, 2 * (n - 1))
                dve.scalar_tensor_tensor(out=G[par][:, i * 256:(i + 1) * 256], in0=th[i % 2][:, :], scalar=1.0,
                                         in1=pj[i][:, 256:512], op0=ALU.add, op1=ALU.mult).then_inc(G_ready, 1)

            def cumulate(n, par):
                dve.wait_ge(es_ready, n + 1)
                wait(dve, E_full, 2 * (n - 1))
                wait(dve, qe_ready, n - 1)
                for b in range(2):
                    c = slice(b * T, (b + 1) * T)
                    dve.tensor_tensor_scan(enzT[par][:, c], esT[par][:, c], esT[par][:, c], 0.0,
                                           ALU.add, ALU.max).then_inc(scan_done, 1)

            def invert(n, par, b):
                dve.wait_ge(scan_done, 2 * n + b + 1)
                c = slice(b * T, (b + 1) * T)
                dve.reciprocal(enzT[par][:, c], enzT[par][:, c]).then_inc(enz_ready, 1)

            def softmax_in(st):
                dve.wait_ge(ok_full, st + 1)
                dve.wait_ge(J_ready, 2 * st + 2)
                wait(dve, pT_full, st)
                wait(dve, ssum_done, st)
                dve.tensor_tensor(sm[:, :], rg[0][:, :], enzJ[:, :], ALU.mult).then_inc(okz_done, 1)
                dve.wait_ge(okz_done, st + 1)
                dve.tensor_reduce(mx[:, :], sm[:, :].rearrange("p (g m) -> p g m", m=M),
                                  AX_X, ALU.max).then_inc(mx_done, 1)

            def softmax_sum(st):
                dve.wait_ge(p_ready, st + 1)
                wait(dve, rs_done, st)
                dve.tensor_reduce(ssum[:, :], sm[:, :].rearrange("p (g m) -> p g m", m=M),
                                  AX_X, ALU.add).then_inc(ssum_done, 1)

            def softmax_inverse(st):
                dve.wait_ge(ssum_done, st + 1)
                wait(dve, scal_done, st)
                dve.reciprocal(rs[:, :], ssum[:, :]).then_inc(rs_done, 1)
                dve.wait_ge(rs_done, st + 1)
                wait(dve, msn_done, st)
                dve.tensor_tensor(rs2[:, :], rs[:, :], rs[:, :], ALU.mult).then_inc(rs2_done, 1)

            def add_share(done, bp, b):
                dve.wait_ge(out_full, 2 * (done - 1) + b + 1)
                wait(dve, acc_done, 2 * (done - 1) + b)
                a = acc[:, bp * NT + 2 * b:bp * NT + 2 * b + 2, :].rearrange("p n c -> p (n c)")
                dve.tensor_tensor(a, rg[1 - b][:, :], a, ALU.add).then_inc(acc_done, 1)

            def gate_poly(st, e):
                dve.wait_ge(ff_sq, 2 * st + e + 1)
                dve.tensor_scalar(ffa[e][:, :], ffa[e][:, :], GELU_A, 1.0, ALU.mult, ALU.add).then_inc(ff_poly, 1)

            def gate_arg(st, e):
                dve.wait_ge(ff_poly, 2 * st + e + 1)
                wait(dve, inter_lo, 2 * (st - 1) + e + 1)
                dve.tensor_tensor(ffb[e][:, :], pj[2 * e][:, :], ffa[e][:, :], ALU.mult).then_inc(ff_arg, 1)

            def gate_gelu(st, e):
                dve.wait_ge(ff_tanh, 2 * st + e + 1)
                dve.scalar_tensor_tensor(out=ffa[e][:, :], in0=ffb[e][:, :], scalar=1.0, in1=pj[2 * e][:, :],
                                         op0=ALU.add, op1=ALU.mult).then_inc(ff_gelu, 1)

            def hidden(st, e):
                dve.wait_ge(ff_gelu, 2 * st + e + 1)
                dve.tensor_tensor(ffb[e][:, :], pj[2 * e + 1][:, :], ffa[e][:, :], ALU.mult).then_inc(inter_done, 1)

            def slot_query(st, par):
                dve.wait_ge(pT_full, st + 1)
                wait(dve, W_full, 4 * st)
                dve.tensor_tensor(qe[:, :], rg[1][:, :], enzT[par][:, :], ALU.mult).then_inc(qe_ready, 1)

            def rope_cos(n, i):
                dve.wait_ge(swapped, 4 * n + i + 1)
                wait(dve, roped, 4 * n + i - 1)
                dve.tensor_tensor(two(ra[i % 2][:, :]), two(pj[i][:, :]), cos, ALU.mult).then_inc(cos_done, 1)

            def rope_sin(n, i):
                dve.tensor_tensor(two(xs[i % 2][:, :]), two(xs[i % 2][:, :]), sin, ALU.mult).then_inc(sin_done, 1)

            def decode(hp):
                dve.wait_ge(packed_in, 16 * hp + 16)
                base = 5 * hp
                dve.tensor_scalar(packed[:, :], packed[:, :], 0xFF, None, ALU.bitwise_and).then_inc(code_step, 1)
                dve.wait_ge(code_step, base + 1)
                dve.scalar_tensor_tensor(out=codes[:, :], in0=packed[:, :], scalar=12, in1=packed[:, :],
                                         op0=ALU.logical_shift_left, op1=ALU.bitwise_or).then_inc(code_step, 1)
                dve.wait_ge(code_step, base + 2)
                dve.tensor_scalar(packed[:, :], codes[:, :], 9, 0x0E000E00, ALU.logical_shift_left,
                                  ALU.bitwise_and).then_inc(code_step, 1)
                dve.tensor_scalar(codes[:, :], codes[:, :], 12, -0x7FFF8000, ALU.logical_shift_left,
                                  ALU.bitwise_and).then_inc(code_step, 1)
                dve.wait_ge(code_step, base + 4)
                dve.tensor_tensor(packed[:, :], packed[:, :], codes[:, :], ALU.bitwise_or).then_inc(code_step, 1)

            def dequantise(hp):
                halves = packed[:, :].bitcast(F16).rearrange("p (n two) -> p n two", two=2)
                dve.wait_ge(code_step, 5 * hp + 5)
                dve.wait_ge(scaled_in, 16 * hp + 16)
                dve.wait_ge(w_lo, 4 * hp + W_QK + 1)
                for k in range(KT):
                    dve.scalar_tensor_tensor(out=mlp_raw[:, k, :], in0=halves[:, 0:512, k], scalar=2.0 ** 14,
                                             in1=scaled[:, 0:512], op0=ALU.mult, op1=ALU.mult).then_inc(mlp_w, 1)
                dve.tensor_scalar(od_raw[:, 0:512], scaled[:, 768:1280], gn[:, 0:1], 0.5,
                                  ALU.mult, ALU.mult).then_inc(out_w, 1)
                for e in range(2):
                    dve.scalar_tensor_tensor(out=od_raw[:, 512 + e * D:512 + (e + 1) * D],
                                             in0=halves[:, 512:768, e], scalar=2.0 ** 13,
                                             in1=scaled[:, 512:768], op0=ALU.mult, op1=ALU.mult).then_inc(out_w, 1)

            def normalise(bp):
                dve.wait_ge(x_in[bp], 16)
                wait(dve, mv_done, NT * bp)
                wait(dve, xn_done, bp)
                for i in range(NT):
                    dve.bn_stats(bns[:, i, :], acc[:, bp * NT + i, :]).then_inc(bn_done, 1)
                for i in range(NT):
                    dve.wait_ge(bn_done, bp * NT + i + 1)
                    if i == 0 and bp:
                        dve.wait_ge(xpow_done, bp)
                    dve.bn_aggr(mv[:, i, :], bns[:, i, :]).then_inc(mv_done, 1)
                dve.wait_ge(mv_done, (bp + 1) * NT)
                dve.tensor_scalar(mse[:, 0:NT], mv[:, :, 1], EPS, None, ALU.add).then_inc(var_done, 1)
                dve.wait_ge(xpow_done, bp + 1)
                if bp:
                    dve.wait_ge(xT_full, KT * bp)
                for i in range(NT):
                    ins = dve.tensor_scalar(xn[:, i, :], acc[:, bp * NT + i, :], mv[:, i, 0:1],
                                            rstd[:, i:i + 1], ALU.subtract, ALU.mult)
                ins.then_inc(xn_done, 1)

            def x_lo(bp):
                for k in range(KT):
                    dve.wait_ge(xh_done, KT * bp + k + 1)
                    dve.tensor_tensor(xl[:, k, tokens(bp)], rg[k][:, :], xh[:, k, tokens(bp)].bitcast(F32),
                                      ALU.subtract).then_inc(xl_done, 1)

            normalise(0)
            x_lo(0)
            normalise(1)
            for i in range(NT):
                gate_g(0, 0, i)
            clip(0, 0, sc[1][:, :])
            x_lo(1)
            cumulate(0, 0)
            invert(0, 0, 0)
            invert(0, 0, 1)
            dve.wait_ge(const_in, 32)
            for i in range(4):
                rope_cos(0, i)
                rope_sin(0, i)
            normalise(2)
            x_lo(2)
            normalise(3)
            decode(0)
            x_lo(3)
            dequantise(0)

            def stage(hp, bp, first, last):
                st = 4 * hp + bp
                par, npar, pbp = bp % 2, (bp + 1) % 2, (bp - 1) % BP
                more = not (isinstance(hp, int) and hp == HP - 1)
                a_args = (A_full, A_diag, At, bp, "A", st)
                w_args = (W_full, W_diag, Wt, bp, "W", st)
                diagonal(*a_args, 0, mask_a, (ok_full, st))
                if not first:
                    sum_squares(st - 1, 1)
                diagonal(*a_args, 1, mask_a, (ok_full, st))
                if not first:
                    norm_arg(st)
                diagonal(*a_args, 2, mask_a, (ok_full, st))
                if not first:
                    gate_o(st, npar)
                diagonal(*a_args, 3, mask_a, (ok_full, st))
                if not last:
                    gate_g(st + 1, npar, 0)
                    clip(st + 1, npar, sc_bank(bp, "S")[:, :])
                    gate_g(st + 1, npar, 1)
                if not first:
                    gated_lo(st, 0)
                    gated_lo(st, 1)
                if not last:
                    gate_g(st + 1, npar, 2)
                    gate_g(st + 1, npar, 3)
                    cumulate(st + 1, npar)
                softmax_in(st)
                if not last:
                    invert(st + 1, npar, 0)
                if not first:
                    add_share(st, pbp, 0)
                if not last:
                    invert(st + 1, npar, 1)
                softmax_sum(st)
                if not first:
                    add_share(st, pbp, 1)
                softmax_inverse(st)
                gate_poly(st, 0)
                gate_arg(st, 0)
                slot_query(st, par)
                gate_gelu(st, 0)
                diagonal(*w_args, 0, mask_w, (o_full, 2 * st))
                hidden(st, 0)
                gate_poly(st, 1)
                diagonal(*w_args, 1, mask_w, (o_full, 2 * st))
                gate_arg(st, 1)
                gate_gelu(st, 1)
                hidden(st, 1)
                if not last:
                    rope_cos(st + 1, 0)
                    rope_sin(st + 1, 0)
                diagonal(*w_args, 2, mask_w, (o_full, 2 * st))
                if not last:
                    rope_cos(st + 1, 1)
                    rope_sin(st + 1, 1)
                diagonal(*w_args, 3, mask_w, (o_full, 2 * st))
                if not last:
                    rope_cos(st + 1, 2)
                    rope_sin(st + 1, 2)
                sum_squares(st, 0)
                if not last:
                    rope_cos(st + 1, 3)
                    rope_sin(st + 1, 3)
                if bp == 1 and more:
                    decode(hp + 1)
                if bp == 3 and more:
                    dequantise(hp + 1)

            each_stage(dve, stage)
            sum_squares(STEPS - 1, 1)
            norm_arg(STEPS)
            gate_o(STEPS, (BP - 1) % 2)
            gated_lo(STEPS, 0)
            gated_lo(STEPS, 1)
            add_share(STEPS, BP - 1, 0)
            add_share(STEPS, BP - 1, 1)

        @block.gpsimd
        def _(pool):
            def split_lo(hp, which):
                pool.wait_ge(w_hi, 4 * hp + which + 1)
                if which == W_VG:
                    dst, src, hi = wvg[1][:, :, :], raw_k[:, :, 512:1024], wvg[0][:, :, :]
                elif which == W_QK:
                    dst, src, hi = wqk[1][:, :, :], raw_k[:, :, 0:512], wqk[0][:, :, :]
                elif which == W_GU:
                    dst, src, hi = wgu[1][:, :, :], mlp_raw, wgu[0][:, :, :]
                else:
                    dst, src, hi = (wod[1][:, :, :].rearrange("p s c -> p (s c)"), od_raw,
                                    wod[0][:, :, :].rearrange("p s c -> p (s c)"))
                pool.tensor_tensor(dst, src, hi.bitcast(F32), ALU.subtract).then_inc(w_lo, 1)

            def rotate(n, i):
                pool.wait_ge(cos_done, 4 * n + i + 1)
                pool.wait_ge(sin_done, 4 * n + i + 1)
                wait(pool, A_full, 4 * n)
                pool.tensor_tensor(qkT[:, i, :], ra[i % 2][:, :], xs[i % 2][:, :], ALU.add).then_inc(roped, 1)

            def norm_pow(done):
                pool.wait_ge(mse_done, done)
                wait(pool, scal_done, done - 1)
                pool.tensor_tensor(rstd[:, :], mse[:, :], mhalf[:, :], ALU.pow).then_inc(pow_done, 1)

            def subtract_max(st):
                pool.wait_ge(mx_done, st + 1)
                s = sm[:, :].rearrange("p (g m) -> p g m", m=M)
                pool.tensor_tensor(s, s, mx[:, :].unsqueeze(2).to_broadcast([P, 8, M]),
                                   ALU.subtract).then_inc(sub_done, 1)

            def hidden_lo(st, e):
                pool.wait_ge(inter_hi, 2 * st + e + 1)
                pool.tensor_tensor(inter[1][e][:, :], ffb[e][:, :], inter[0][e][:, :].bitcast(F32),
                                   ALU.subtract).then_inc(inter_lo, 1)

            pool.memset(mhalf[:, :], -0.5)
            pool.memset(ident[:, :], 0.0)
            pool.memset(mask_a[:, :, :], SCALE).then_inc(const_set, 1)
            pool.memset(mask_w[:, :, :], 1.0).then_inc(const_set, 1)
            pool.memset(h1[:, :], 1.0).then_inc(const_set, 2)
            pool.wait_ge(const_set, 4)
            pool.affine_select(out=ident[:, :], in_=ident[:, :], compare_op=ALU.not_equal, fill=1.0, base=0,
                               pattern=[[-1, P]], channel_multiplier=1)
            for m in (mask_a, mask_w):
                ins = pool.affine_select(out=m[:, :, :], in_=m[:, :, :], compare_op=ALU.is_ge, fill=0.0, base=0,
                                         pattern=[[0, 2], [1, P]], channel_multiplier=-1)
            ins.then_inc(consts, 1)

            def x_pow(bp):
                pool.wait_ge(var_done, bp + 1)
                if bp:
                    pool.wait_ge(xn_done, bp)
                pool.tensor_tensor(rstd[:, 0:NT], mse[:, 0:NT], mhalf[:, 0:NT], ALU.pow).then_inc(xpow_done, 1)

            x_pow(0)
            pool.wait_ge(ws1_hi, 1)
            pool.tensor_tensor(ws1_s[1], ws1, ws1_s[0].bitcast(F32), ALU.subtract).then_inc(ws1_lo, 1)
            split_lo(0, W_VG)
            x_pow(1)
            split_lo(0, W_QK)
            for i in range(4):
                rotate(0, i)
            x_pow(2)
            x_pow(3)
            split_lo(0, W_GU)

            def stage(hp, bp, first, last):
                st = 4 * hp + bp
                more = not (isinstance(hp, int) and hp == HP - 1)
                if not first:
                    norm_pow(st)
                subtract_max(st)
                if first:
                    split_lo(0, W_OD)
                if bp == 2 and more:
                    split_lo(hp + 1, W_VG)
                hidden_lo(st, 0)
                hidden_lo(st, 1)
                if not last:
                    for i in range(4):
                        rotate(st + 1, i)
                if bp == 2 and more:
                    split_lo(hp + 1, W_QK)
                if bp == 3 and more:
                    split_lo(hp + 1, W_GU)
                if bp == 0 and not first:
                    split_lo(hp, W_OD)

            each_stage(pool, stage)
            norm_pow(STEPS)


def lay_out(a):
    c = np.ascontiguousarray

    def heads(w):
        return w.reshape(HP, 2, P, P, KT).transpose(0, 3, 4, 1, 2)

    q, k, v, g = (heads(a[f"L0_attn_{n}"]) for n in ("Wq", "Wk", "Wv", "Wg"))
    qk = np.stack([q, k], axis=4).reshape(HP, P, KT, 512)
    vg = np.stack([v, g], axis=3).reshape(HP, P, KT, 512)
    qkvg = np.concatenate([qk, vg], axis=3).reshape(HP, P, KT * 1024)

    def units(w):
        return w.reshape(HP, P, 2, w.shape[1]).transpose(0, 3, 2, 1).reshape(HP, w.shape[1], 2 * P)

    down = a["L0_ffn_down_W_packed"].reshape(D, HP, P).transpose(1, 2, 0)
    packed = np.concatenate([units(a["L0_ffn_gate_W_packed"]), units(a["L0_ffn_up_W_packed"]), down], axis=2)
    rep = P // (D // 32)
    gs, us = (np.repeat(units(a[f"L0_ffn_{n}_scales"]), rep, axis=1) for n in ("gate", "up"))
    ds = np.repeat(a["L0_ffn_down_scales"].reshape(D, HP, 8).transpose(1, 2, 0), rep, axis=1)
    wo = a["L0_attn_Wo"].reshape(D, HP, 2, P).transpose(1, 3, 2, 0).reshape(HP, P, 2 * D)
    scaled = np.concatenate([gs, us, ds, wo], axis=2)
    slot = np.concatenate([a["L0_attn_Ws2"].reshape(HP, P, RANK).transpose(0, 2, 1),
                           a["L0_attn_bs2"].reshape(HP, 1, P)], axis=1)
    slot1 = np.zeros((P, KT, P), a["L0_attn_Ws1"].dtype)
    slot1[:, :, 0:RANK] = a["L0_attn_Ws1"].reshape(RANK, P, KT).transpose(1, 2, 0)
    return {"x": c(a["L0_attn_hidden_states"]), "w_qkvg": c(qkvg), "w_packed": c(packed), "w_scaled": c(scaled),
            "w_slot": c(slot), "w_slot1": slot1, "g_norm": c(a["L0_attn_g_norm_weight"].reshape(P, 1))}


def rope_table():
    pos = np.arange(T, dtype=np.float32)
    inv = (1.0 / np.power(np.float32(10000.0), np.arange(0, DK, 2, dtype=np.float32) / np.float32(DK))).astype(np.float32)
    ang = inv[:, None] * pos[None, :]
    cos, sin = np.cos(ang).astype(np.float32), np.sin(ang).astype(np.float32)
    return np.ascontiguousarray(np.stack([np.concatenate([cos, cos]), np.concatenate([-sin, sin])], axis=1))


def kernel(**inputs):
    import concourse.bacc as _bacc
    from concourse.bass_utils import run_bass_kernel_spmd as _run

    nc = _bacc.Bacc("TRN2", target_bir_lowering=False, num_devices=1)
    arrays = lay_out({n: np.asarray(a) for n, a in inputs.items()})
    arrays["rope_tab"] = rope_table()
    args = [nc.dram_tensor(f"in_{n}", a.shape, mybir.dt.from_np(a.dtype), kind="ExternalInput").ap()
            for n, a in arrays.items()]
    out = nc.dram_tensor("out_0", (B, T, D), F32, kind="ExternalOutput").ap()
    build(nc, *args, out)
    r = _run(nc, [{f"in_{n}": a for n, a in arrays.items()}], core_ids=[0])
    return r.results[0]["out_0"]
```

```python
from contextlib import ExitStack

import numpy as np

import concourse.bass as bass
from concourse import mybir

F32 = mybir.dt.float32
F32R = mybir.dt.float32r
F16 = mybir.dt.float16
I32 = mybir.dt.int32
ALU = mybir.AluOpType
ACT = mybir.ActivationFunctionType
AX_X = mybir.AxisListType.X

P = 128
B, T, D = 8, 256, 256
H, DK, DV, M = 16, 128, 128, 64
RANK = 16
MLP = 2048
HP = H // 2
BP = B // 2
TOK = 2 * T
KT = D // P
NT = TOK // P
NF = MLP // HP
EPS = 1e-5
CLAMP = 32.0
SCALE = DK ** -0.5
GELU_A, GELU_C = 0.044715, 0.7978845608028654
STEPS = HP * BP
GROUP = 32
SLOT_K = 3 * GROUP
W_VG, W_QK, W_GU, W_OD = range(4)
SC_SLOTS = {"A": (0, 1, 2, 3), "S": (4,), "W": (5, 6, 7, 8), "E": (9, 10)}
SC_STEP = 11


def build(nc, x, w_qkvg, w_packed, w_scaled, w_slot, w_slot1, g_norm, rope_tab, out):
    with ExitStack() as ctx:
        def sb(name, shape, dt=F32):
            return ctx.enter_context(nc.sbuf_tensor(name, shape, dt))

        def sem(name):
            return ctx.enter_context(nc.semaphore(name))

        acc = sb("acc", [P, BP * NT, D])
        xh = sb("xh", [P, KT, B * T], F32R)
        xl = sb("xl", [P, KT, B * T], F32R)
        wqk = [sb(f"wqk_{s}", [P, KT, 512], F32R) for s in ("hi", "lo")]
        wvg = [sb(f"wvg_{s}", [P, KT, 512], F32R) for s in ("hi", "lo")]
        wgu = [sb(f"wgu_{s}", [P, KT, 512], F32R) for s in ("hi", "lo")]
        wod = [sb(f"wod_{s}", [P, 4, D], F32R) for s in ("hi", "lo")]
        raw = sb("raw", [P, KT * 1024])
        packed = sb("packed", [P, 768], I32)
        codes = sb("codes", [P, 768], I32)
        scaled = sb("scaled", [P, 1280])
        ws2_raw = sb("ws2_raw", [SLOT_K, P])
        ws2 = sb("ws2", [SLOT_K, P], F32R)
        h1 = sb("h1", [SLOT_K, BP, TOK], F32R)
        gn = sb("gn", [P, 1])
        rope = sb("rope", [P, 2, T])
        mask_a = sb("mask_a", [P, 2, P])
        mask_w = sb("mask_w", [P, 2, P])
        ident = sb("ident", [P, P])
        esT = [sb(f"esT{i}", [P, TOK]) for i in range(2)]
        enzT = [sb(f"enzT{i}", [P, TOK]) for i in range(2)]
        esJ = sb("esJ", [P, NT, P])
        enzJ = sb("enzJ", [P, TOK])
        qkT = sb("qkT", [P, 4, TOK])
        xs = [sb(f"xs{i}", [P, TOK]) for i in range(2)]
        ra = [sb(f"ra{i}", [P, TOK]) for i in range(2)]
        vS = [sb(f"vS{i}", [P, NT, 256]) for i in range(2)]
        G = [sb(f"G{i}", [P, NT * 256]) for i in range(2)]
        th = [sb(f"th{i}", [P, 256]) for i in range(2)]
        At = [sb(f"At{i}", [P, 3, P]) for i in range(4)]
        Wt = [sb(f"Wt{i}", [P, 3, P]) for i in range(4)]
        sm = sb("sm", [P, TOK])
        qe = sb("qe", [P, TOK])
        osq = sb("osq", [P, TOK])
        og = sb("og", [P, NT * 256])
        ogT = [[sb(f"ogT_{s}{h}", [P, TOK], F32R) for h in range(2)] for s in ("hi", "lo")]
        inter = [[sb(f"inter_{s}{e}", [P, TOK], F32R) for e in range(2)] for s in ("hi", "lo")]
        ffa = [sb(f"ffa{i}", [P, TOK]) for i in range(2)]
        ffb = [sb(f"ffb{i}", [P, TOK]) for i in range(2)]
        mx = sb("mx", [P, 8])
        ssum = sb("ssum", [P, 8])
        rs = sb("rs", [P, 8])
        rs2 = sb("rs2", [P, 8])
        ms = sb("ms", [P, 8])
        msn = sb("msn", [P, 8])
        mse = sb("mse", [P, 8])
        rstd = sb("rstd", [P, 8])
        scal = sb("scal", [P, 8])
        mhalf = sb("mhalf", [P, 8])
        bns = sb("bns", [P, NT, 6])
        mv = sb("mv", [P, NT, 2])

        bank = [ctx.enter_context(nc.psum_tensor(f"bank{i}", [P, 512], F32)) for i in range(8)]
        pj = bank[0:4]
        sc = bank[4:6]
        rg = bank[6:8]

        x_in = [sem(f"x_in{i}") for i in range(BP)]
        raw_in, packed_in, scaled_in, ws2_in = sem("raw_in"), sem("packed_in"), sem("scaled_in"), sem("ws2_in")
        ws1_in, const_in, out_sent = sem("ws1_in"), sem("const_in"), sem("out_sent")
        A_full, S_full, W_full, E_full = sem("A_full"), sem("S_full"), sem("W_full"), sem("E_full")
        ok_full, pT_full, o_full, ogT_full, out_full = (
            sem("ok_full"), sem("pT_full"), sem("o_full"), sem("ogT_full"), sem("out_full"))
        vg_full, qk_full, ffn_full = sem("vg_full"), sem("qk_full"), sem("ffn_full")
        xT_full, h1_full = sem("xT_full"), sem("h1_full")
        ws2_hi = sem("ws2_hi")
        scales_set, out_w, gn_half = sem("scales_set"), sem("out_w"), sem("gn_half")
        A_off, W_off, v_ready, gtanh, p_ready, osq_done = (
            sem("A_off"), sem("W_off"), sem("v_ready"), sem("gtanh"), sem("p_ready"), sem("osq_done"))
        ogT_hi, ff_sq, ff_tanh, inter_hi = sem("ogT_hi"), sem("ff_sq"), sem("ff_tanh"), sem("inter_hi")
        swapped, es_ready, J_ready, w_hi = sem("swapped"), sem("es_ready"), sem("J_ready"), sem("w_hi")
        xh_done, h1_done, ws1_hi = sem("xh_done"), sem("h1_done"), sem("ws1_hi")
        A_diag, W_diag, G_ready, okz_done, mx_done = (
            sem("A_diag"), sem("W_diag"), sem("G_ready"), sem("okz_done"), sem("mx_done"))
        ssum_done, rs_done, rs2_done, ms_done, msn_done, mse_done, scal_done = (
            sem("ssum_done"), sem("rs_done"), sem("rs2_done"), sem("ms_done"), sem("msn_done"),
            sem("mse_done"), sem("scal_done"))
        og_done, ogT_lo, acc_done, qe_ready = sem("og_done"), sem("ogT_lo"), sem("acc_done"), sem("qe_ready")
        ff_arg, ff_gelu, inter_done = sem("ff_arg"), sem("ff_gelu"), sem("inter_done")
        cos_done, sin_done, clip_done, scan_done, enz_ready = (
            sem("cos_done"), sem("sin_done"), sem("clip_done"), sem("scan_done"), sem("enz_ready"))
        code_step = sem("code_step")
        ws2_lo, h1_lo = sem("ws2_lo"), sem("h1_lo")
        bn_done, mv_done, var_done, xn_done, xl_done = (
            sem("bn_done"), sem("mv_done"), sem("var_done"), sem("xn_done"), sem("xl_done"))
        mlp_w, down_w = sem("mlp_w"), sem("down_w")
        roped, sub_done, inter_lo, pow_done, w_lo = (
            sem("roped"), sem("sub_done"), sem("inter_lo"), sem("pow_done"), sem("w_lo"))
        const_set, consts, ws1_lo, xpow_done = sem("const_set"), sem("consts"), sem("ws1_lo"), sem("xpow_done")

        x_rows = x.rearrange("b (n p) d -> p (b n) d", p=P)
        out_rows = out.rearrange("b (n p) d -> p (b n) d", p=P)
        raw_k = raw[:, :].rearrange("p (k n) -> p k n", k=KT)
        mlp_raw = raw[:, 0:1024].rearrange("p (k n) -> p k n", k=KT)
        od_raw = raw[:, 1024:2048]
        xn = [og[:, :].rearrange("p (n d) -> p n d", n=NT), G[1][:, :].rearrange("p (n d) -> p n d", n=NT),
              vS[1][:, :, :], og[:, :].rearrange("p (n d) -> p n d", n=NT)]
        ws1 = osq[:, 0:KT * P].rearrange("p (k n) -> p k n", k=KT)
        ws1_s = [ogT[s][0][:, 0:KT * P].rearrange("p (k n) -> p k n", k=KT) for s in range(2)]
        xhl = (xh, xl)

        def wait(eng, s, value):
            if not isinstance(value, int) or value > 0:
                eng.wait_ge(s, value)

        def tokens(bp, tile=None):
            return slice(bp * TOK, (bp + 1) * TOK) if tile is None else slice(
                bp * TOK + tile * P, bp * TOK + (tile + 1) * P)

        def sc_bank(bp, kind, i=0):
            return sc[(SC_STEP * bp + SC_SLOTS[kind][i]) % 2]

        def each_stage(eng, stage):
            for bp in range(BP):
                stage(0, bp, bp == 0, False)
            with eng.Fori(1, HP - 1) as hp:
                for bp in range(BP):
                    stage(hp, bp, False, False)
            for bp in range(BP):
                stage(HP - 1, bp, False, bp == BP - 1)

        def three(pe, dst, stat, mov, start, stop):
            pe.matmul(dst, stat[0], mov[0], start=start, stop=False)
            pe.matmul(dst, stat[0], mov[1], start=False, stop=False)
            return pe.matmul(dst, stat[1], mov[0], start=False, stop=stop)

        block = ctx.enter_context(nc.Block())

        @block.sync
        def _(sp):
            for bp in range(BP):
                sp.dma_start(acc[:, bp * NT:(bp + 1) * NT, :],
                             x_rows[:, bp * NT:(bp + 1) * NT, :]).then_inc(x_in[bp], 16)
                if bp == 0:
                    sp.dma_start(ws1, w_slot1).then_inc(ws1_in, 16)
                    sp.dma_start(raw[:, :], w_qkvg[0]).then_inc(raw_in, 16)
                    sp.dma_start(ws2_raw[:, :], w_slot[0]).then_inc(ws2_in, 16)
                    sp.dma_start(rope[:, :, :], rope_tab).then_inc(const_in, 16)
                    sp.dma_start(gn[:, :], g_norm).then_inc(const_in, 16)
                if bp == 1:
                    sp.dma_start(packed[:, :], w_packed[0]).then_inc(packed_in, 16)
                    sp.dma_start(scaled[:, :], w_scaled[0]).then_inc(scaled_in, 16)
            with sp.Fori(0, HP - 1) as hp:
                sp.wait_ge(w_lo, 4 * hp + 4)
                sp.wait_ge(ws2_lo, 4 * hp + 4)
                sp.dma_start(ws2_raw[:, :], w_slot[hp + 1]).then_inc(ws2_in, 16)
                sp.dma_start(raw[:, :], w_qkvg[hp + 1]).then_inc(raw_in, 16)
                sp.dma_start(packed[:, :], w_packed[hp + 1]).then_inc(packed_in, 16)
                sp.dma_start(scaled[:, :], w_scaled[hp + 1]).then_inc(scaled_in, 16)
            for bp in range(BP):
                sp.wait_ge(acc_done, 2 * ((HP - 1) * BP + bp + 1))
                sp.dma_start(out_rows[:, bp * NT:(bp + 1) * NT, :],
                             acc[:, bp * NT:(bp + 1) * NT, :]).then_inc(out_sent, 16)
            sp.wait_ge(out_sent, 16 * BP)

        @block.tensor
        def _(pe):
            def project_vg(n, bp, hp, i, free):
                if i == 0:
                    wait(pe, w_lo, 4 * hp + W_VG + 1)
                if free:
                    pe.wait_ge(ff_gelu if i % 2 == 0 else inter_done, 2 * (n - 1) + i // 2 + 1)
                for k in range(KT):
                    mm = three(pe, pj[i][:, :], [a[:, k, tokens(bp, i)] for a in xhl],
                               [w[:, k, :] for w in wvg], k == 0, k == KT - 1)
                mm.then_inc(vg_full, 1)

            def project_qk(n, bp, hp, i):
                if i == 0:
                    wait(pe, w_lo, 4 * hp + W_QK + 1)
                pe.wait_ge(G_ready, 4 * n + i + 1)
                for k in range(KT):
                    mm = three(pe, pj[i][:, :], [w[:, k, i * P:(i + 1) * P] for w in wqk],
                               [a[:, k, tokens(bp)] for a in xhl], k == 0, k == KT - 1)
                mm.then_inc(qk_full, 1)

            def mlp_up(st, bp, hp, i):
                if i == 0:
                    wait(pe, w_lo, 4 * hp + W_GU + 1)
                pe.wait_ge(cos_done, 4 * st + i + 1)
                col = (i % 2 * 2 + i // 2) * P
                for k in range(KT):
                    mm = three(pe, pj[i][:, :], [w[:, k, col:col + P] for w in wgu],
                               [a[:, k, tokens(bp)] for a in xhl], k == 0, k == KT - 1)
                mm.then_inc(ffn_full, 1)

            def slot_scores(n, bp, hp):
                if bp == 0:
                    pe.wait_ge(ws2_lo, 4 * hp + 4)
                pe.matmul(sc_bank((bp - 1) % BP, "S")[:, :] if n is not None else sc[1][:, :],
                          ws2[:, :], h1[:, bp, :], start=True, stop=True).then_inc(S_full, 1)

            def slot_transpose(dst, src):
                for i in range(NT):
                    mm = pe.transpose(dst[:, i * P:(i + 1) * P], src[:, i * P:(i + 1) * P], ident[:, :])
                mm.then_inc(E_full, 1)

            def scores(st, bp, i, hp):
                h, b = i // 2, i % 2
                if b == 0:
                    pe.wait_ge(roped, 4 * st + 2 * h + 2)
                dst = sc_bank(bp, "A", i)
                t0 = b * T
                pe.matmul(dst[:, 0:T], qkT[:, 2 * h + 1, t0:t0 + P], qkT[:, 2 * h, t0:t0 + T],
                          start=True, stop=True)
                pe.matmul(dst[:, T:T + P], qkT[:, 2 * h + 1, t0 + P:t0 + T], qkT[:, 2 * h, t0 + P:t0 + T],
                          start=True, stop=True).then_inc(A_full, 1)

            def slot_reads(st):
                pe.wait_ge(A_off, 4 * st + 4)
                pe.wait_ge(J_ready, 2 * st + 1)
                for b in range(2):
                    for h in range(2):
                        a = At[2 * h + b]
                        c = b * 256 + h * M
                        pe.matmul(rg[0][:, c:c + M], a[:, 0, :], esJ[:, 2 * b, h * M:(h + 1) * M],
                                  start=True, stop=True)
                        c += P
                        pe.matmul(rg[0][:, c:c + M], a[:, 1, :], esJ[:, 2 * b, h * M:(h + 1) * M],
                                  start=True, stop=False)
                        mm = pe.matmul(rg[0][:, c:c + M], a[:, 2, :], esJ[:, 2 * b + 1, h * M:(h + 1) * M],
                                       start=False, stop=True)
                mm.then_inc(ok_full, 1)

            def slot_weights(st, bp, i):
                h, b = i // 2, i % 2
                dst = sc_bank(bp, "W", i)
                g = slice(h * M, (h + 1) * M)
                t0 = b * T
                pe.matmul(dst[:, 0:T], esT[bp % 2][g, t0:t0 + P], qe[g, t0:t0 + T], start=True, stop=True)
                pe.matmul(dst[:, T:T + P], esT[bp % 2][g, t0 + P:t0 + T], qe[g, t0 + P:t0 + T],
                          start=True, stop=True).then_inc(W_full, 1)

            def values(st, bp, b):
                for h in range(2):
                    pe.wait_ge(W_off, 4 * st + 2 * h + b + 1)
                    w = Wt[2 * h + b]
                    v0 = vS[bp % 2][:, 2 * b, h * DV:(h + 1) * DV]
                    v1 = vS[bp % 2][:, 2 * b + 1, h * DV:(h + 1) * DV]
                    c = h * DV
                    pe.matmul(rg[b][:, c:c + DV], w[:, 0, :], v0, start=True, stop=True)
                    c += 256
                    pe.matmul(rg[b][:, c:c + DV], w[:, 1, :], v0, start=True, stop=False)
                    mm = pe.matmul(rg[b][:, c:c + DV], w[:, 2, :], v1, start=False, stop=True)
                mm.then_inc(o_full, 1)

            def gated_transpose(done):
                pe.wait_ge(og_done, 2 * done)
                for h in range(2):
                    for i in range(NT):
                        mm = pe.transpose(rg[h][:, i * P:(i + 1) * P],
                                          og[:, i * 256 + h * DV:i * 256 + (h + 1) * DV], ident[:, :])
                    mm.then_inc(ogT_full, 1)

            def outputs(done, b, hp, free_okz):
                if b == 0:
                    pe.wait_ge(ogT_hi, 2 * done)
                    pe.wait_ge(ogT_lo, 2 * done)
                    pe.wait_ge(inter_lo, 2 * done)
                    wait(pe, w_lo, 4 * hp + W_OD + 1)
                elif free_okz is not None:
                    pe.wait_ge(okz_done, free_okz)
                for tt in range(2):
                    cols = slice((2 * b + tt) * P, (2 * b + tt + 1) * P)
                    for s in range(4):
                        src = ogT if s < 2 else inter
                        mm = three(pe, rg[1 - b][:, tt * D:(tt + 1) * D],
                                   [src[u][s % 2][:, cols] for u in range(2)],
                                   [w[:, s, :] for w in wod], s == 0, s == 3)
                mm.then_inc(out_full, 1)

            def transpose_x(bp):
                pe.wait_ge(xn_done, bp + 1)
                for k in range(KT):
                    if bp == 1:
                        pe.wait_ge(xh_done, k + 1)
                        pe.wait_ge(xl_done, k + 1)
                    if bp == 2 and k == 0:
                        pe.wait_ge(h1_done, 4)
                        pe.wait_ge(h1_lo, 2)
                    if bp == 2 and k == 1:
                        pe.wait_ge(J_ready, 2)
                    if bp == 3 and k == 0:
                        pe.wait_ge(okz_done, 1)
                    if bp == 3 and k == 1:
                        pe.wait_ge(qe_ready, 1)
                    for i in range(NT):
                        mm = pe.transpose(rg[k][:, i * P:(i + 1) * P], xn[bp][:, i, k::KT], ident[:, :])
                    mm.then_inc(xT_full, 1)

            def slot_inner(bp, dst):
                pe.wait_ge(xl_done, KT * (bp + 1))
                pe.wait_ge(xh_done, KT * (bp + 1))
                for k in range(KT):
                    mm = three(pe, dst[:, :], [w[:, k, :] for w in ws1_s],
                               [a[:, k, tokens(bp)] for a in xhl], k == 0, k == KT - 1)
                mm.then_inc(h1_full, 1)

            pe.wait_ge(consts, 1)
            transpose_x(0)
            pe.wait_ge(ws1_lo, 1)
            slot_inner(0, sc[0])
            for i in range(NT):
                if i == 3:
                    pe.wait_ge(h1_lo, 1)
                    pe.wait_ge(h1_done, 2)
                    slot_scores(None, 0, 0)
                project_vg(0, 0, 0, i, False)
            transpose_x(1)
            project_qk(0, 0, 0, 0)
            project_qk(0, 0, 0, 1)
            pe.wait_ge(es_ready, 1)
            slot_transpose(sc[0], esT[0])
            project_qk(0, 0, 0, 2)
            slot_inner(1, rg[0])
            project_qk(0, 0, 0, 3)

            def stage(hp, bp, first, last):
                st = 4 * hp + bp
                nbp = (bp + 1) % BP
                nhp = hp + 1 if bp == BP - 1 else hp
                php = hp - 1 if bp == 0 else hp
                for i in (0, 1):
                    if first and i == 1:
                        pe.wait_ge(clip_done, 1)
                    else:
                        pe.wait_ge(J_ready, 2 * st + i + 1)
                    scores(st, bp, i, hp)
                mlp_up(st, bp, hp, 0)
                mlp_up(st, bp, hp, 1)
                for i in (2, 3):
                    pe.wait_ge(A_off, 4 * st + i - 1)
                    scores(st, bp, i, hp)
                if first:
                    pe.wait_ge(enz_ready, 2)
                    slot_transpose(rg[1], enzT[0])
                mlp_up(st, bp, hp, 2)
                mlp_up(st, bp, hp, 3)
                if not first:
                    gated_transpose(st)
                if not last:
                    pe.wait_ge(A_off, 4 * st + 3)
                    slot_scores(st, nbp, nhp)
                if not last:
                    project_vg(st + 1, nbp, nhp, 0, True)
                if first:
                    transpose_x(2)
                if not last:
                    project_vg(st + 1, nbp, nhp, 1, True)
                if first:
                    slot_inner(2, rg[1])
                else:
                    pe.wait_ge(ogT_hi, 2 * st - 1)
                    pe.wait_ge(ogT_lo, 2 * st - 1)
                slot_reads(st)
                if not first:
                    outputs(st, 0, php, None)
                if not last:
                    project_vg(st + 1, nbp, nhp, 2, True)
                if not first:
                    outputs(st, 1, php, st + 1)
                if not last:
                    project_vg(st + 1, nbp, nhp, 3, True)
                pe.wait_ge(p_ready, st + 1)
                if first:
                    pe.wait_ge(h1_done, 6)
                    pe.wait_ge(h1_lo, 3)
                else:
                    pe.wait_ge(acc_done, 2 * st - 1)
                for i in range(NT):
                    mm = pe.transpose(rg[1][:, i * P:(i + 1) * P], sm[:, i * P:(i + 1) * P], ident[:, :])
                mm.then_inc(pT_full, 1)
                if not last:
                    project_qk(st + 1, nbp, nhp, 0)
                for i in range(4):
                    if not last and i != 1:
                        project_qk(st + 1, nbp, nhp, max(i, 1))
                    if first and i == 2:
                        transpose_x(3)
                    if i == 0:
                        pe.wait_ge(qe_ready, st + 1)
                        pe.wait_ge(A_off, 4 * st + 4)
                    elif i > 1:
                        pe.wait_ge(W_off, 4 * st + i - 1)
                    elif not last:
                        pe.wait_ge(clip_done, st + 2)
                    slot_weights(st, bp, i)
                pe.wait_ge(v_ready, 4 * st + 4)
                if first:
                    slot_inner(3, rg[1])
                else:
                    pe.wait_ge(acc_done, 2 * st)
                values(st, bp, 0)
                if not last:
                    pe.wait_ge(es_ready, st + 2)
                    slot_transpose(sc_bank(bp, "E", 0), esT[nbp % 2])
                    pe.wait_ge(W_off, 4 * st + 4)
                    pe.wait_ge(enz_ready, 2 * (st + 2))
                    slot_transpose(sc_bank(bp, "E", 1), enzT[nbp % 2])
                if first:
                    pe.wait_ge(h1_done, 8)
                    pe.wait_ge(h1_lo, 4)
                values(st, bp, 1)

            each_stage(pe, stage)
            gated_transpose(STEPS)
            outputs(STEPS, 0, HP - 1, None)
            outputs(STEPS, 1, HP - 1, None)

        @block.scalar
        def _(act):
            def split_hi(hp, which):
                if which == W_VG:
                    wait(act, vg_full, 16 * hp)
                    act.wait_ge(raw_in, 16 * hp + 16)
                    dst, src = wvg[0][:, :, :], raw_k[:, :, 512:1024]
                elif which == W_QK:
                    wait(act, qk_full, 16 * hp)
                    act.wait_ge(raw_in, 16 * hp + 16)
                    dst, src = wqk[0][:, :, :], raw_k[:, :, 0:512]
                elif which == W_GU:
                    wait(act, ffn_full, 16 * hp)
                    act.wait_ge(mlp_w, 2 * hp + 2)
                    dst, src = wgu[0][:, :, :], mlp_raw
                else:
                    wait(act, out_full, 8 * hp)
                    act.wait_ge(out_w, hp + 1)
                    act.wait_ge(down_w, 2 * hp + 2)
                    dst, src = wod[0][:, :, :].rearrange("p s c -> p (s c)"), od_raw
                act.activation(dst, src, ACT.Copy).then_inc(w_hi, 1)

            def prepare_scales(hp):
                act.wait_ge(scaled_in, 16 * hp + 16)
                act.activation(scaled[:, 0:512], scaled[:, 0:512], ACT.Copy, scale=2.0 ** 14)
                act.activation(scaled[:, 512:768], scaled[:, 512:768], ACT.Copy, scale=2.0 ** 13).then_inc(scales_set, 1)

            def prepare_out(hp):
                act.wait_ge(w_lo, 4 * hp + W_QK + 1)
                act.activation(od_raw[:, 0:512], scaled[:, 768:1280], ACT.Copy, scale=gn[:, 0:1]).then_inc(out_w, 1)

            def split_slot(hp):
                wait(act, S_full, BP * hp)
                act.wait_ge(ws2_in, 16 * hp + 16)
                act.activation(ws2[:, :], ws2_raw[:, :], ACT.Copy).then_inc(ws2_hi, 1)

            def copy_v(n, par, i):
                act.wait_ge(vg_full, 4 * n + i + 1)
                if i == 0:
                    wait(act, o_full, 2 * (n - 1))
                act.activation(vS[par][:, i, :], pj[i][:, 0:256], ACT.Copy).then_inc(v_ready, 1)
                wait(act, G_ready, 4 * n + i - 1)
                act.activation(th[i % 2][:, :], pj[i][:, 256:512], ACT.Tanh, scale=0.5).then_inc(gtanh, 1)

            def swap_halves(n, i):
                act.wait_ge(qk_full, 4 * n + i + 1)
                wait(act, roped, 4 * n + i - 1)
                act.activation(xs[i % 2][0:64, :], pj[i][64:128, :], ACT.Copy)
                act.activation(xs[i % 2][64:128, :], pj[i][0:64, :], ACT.Copy).then_inc(swapped, 1)

            def slot_exp(n, par):
                act.wait_ge(clip_done, n + 1)
                act.activation(esT[par][:, :], esT[par][:, :], ACT.Exp).then_inc(es_ready, 1)

            def copy_J(n, which, src):
                act.wait_ge(E_full, 2 * n + which + 1)
                if which == 0:
                    wait(act, ok_full, n)
                    act.activation(esJ[:, :, :].rearrange("p n m -> p (n m)"), src, ACT.Copy).then_inc(J_ready, 1)
                else:
                    wait(act, okz_done, n)
                    act.activation(enzJ[:, :], src, ACT.Copy).then_inc(J_ready, 1)

            def off_diagonal(diag, done, dst, bp, kind, st, i, scale):
                act.wait_ge(diag, 4 * st + i + 1)
                act.activation(dst[i][:, 1, :], sc_bank(bp, kind, i)[:, P:2 * P], ACT.Copy,
                               scale=scale).then_inc(done, 1)

            def square_o(st, b):
                act.wait_ge(o_full, 2 * st + b + 1)
                wait(act, ms_done, 2 * st + b)
                act.activation(osq[:, :], rg[b][:, :], ACT.Square).then_inc(osq_done, 1)

            def gated_hi(done, h):
                act.wait_ge(ogT_full, 2 * (done - 1) + h + 1)
                wait(act, out_full, 2 * (done - 1))
                act.activation(ogT[0][h][:, :], rg[h][:, :], ACT.Copy).then_inc(ogT_hi, 1)

            def gate_square(st, e):
                act.wait_ge(ffn_full, 4 * st + 2 * e + 1)
                wait(act, inter_done, 2 * (st - 1) + e + 1)
                act.activation(ffa[e][:, :], pj[2 * e][:, :], ACT.Square,
                               scale=GELU_A ** 0.5).then_inc(ff_sq, 1)

            def gate_tanh(st, e):
                act.wait_ge(ff_arg, 2 * st + e + 1)
                act.activation(ffb[e][:, :], ffb[e][:, :], ACT.Tanh, scale=GELU_C).then_inc(ff_tanh, 1)

            def hidden_hi(st, e):
                act.wait_ge(inter_done, 2 * st + e + 1)
                wait(act, out_full, 2 * st)
                act.activation(inter[0][e][:, :], ffb[e][:, :], ACT.Copy).then_inc(inter_hi, 1)

            def x_hi(bp):
                for k in range(KT):
                    act.wait_ge(xT_full, KT * bp + k + 1)
                    act.activation(xh[:, k, tokens(bp)], rg[k][:, :], ACT.Copy).then_inc(xh_done, 1)

            def inner_copy(bp, src):
                act.wait_ge(h1_full, bp + 1)
                for g in range(2):
                    rows = slice(g * GROUP, g * GROUP + RANK)
                    act.activation(h1[rows, bp, :], src[rows, :], ACT.Copy).then_inc(h1_done, 1)

            act.wait_ge(ws1_in, 16)
            for k in range(KT):
                ins = act.activation(ws1_s[0][:, k, :], ws1[:, k, :], ACT.Copy)
            ins.then_inc(ws1_hi, 1)
            act.wait_ge(const_set, 4)
            split_hi(0, W_VG)
            x_hi(0)
            split_slot(0)
            inner_copy(0, sc[0])
            split_hi(0, W_QK)
            prepare_scales(0)
            copy_v(0, 0, 0)
            copy_v(0, 0, 1)
            copy_v(0, 0, 2)
            slot_exp(0, 0)
            copy_v(0, 0, 3)
            act.wait_ge(const_in, 32)
            act.activation(gn[:, :], gn[:, :], ACT.Copy, scale=0.5).then_inc(gn_half, 1)
            act.wait_ge(gn_half, 1)
            prepare_out(0)
            x_hi(1)
            swap_halves(0, 0)
            swap_halves(0, 1)
            copy_J(0, 0, sc[0][:, :])
            split_hi(0, W_GU)
            swap_halves(0, 2)
            inner_copy(1, rg[0])
            swap_halves(0, 3)

            def stage(hp, bp, first, last):
                st = 4 * hp + bp
                npar = (bp + 1) % 2
                a_args = (A_diag, A_off, At, bp, "A", st)
                w_args = (W_diag, W_off, Wt, bp, "W", st)
                more = not (isinstance(hp, int) and hp == HP - 1)
                off_diagonal(*a_args, 0, SCALE)
                off_diagonal(*a_args, 1, SCALE)
                gate_square(st, 0)
                gate_tanh(st, 0)
                if bp == 1:
                    split_hi(hp, W_OD)
                if bp == 3 and more:
                    split_hi(hp + 1, W_VG)
                off_diagonal(*a_args, 2, SCALE)
                off_diagonal(*a_args, 3, SCALE)
                if first:
                    copy_J(0, 1, rg[1][:, :])
                gate_square(st, 1)
                if not first:
                    gated_hi(st, 0)
                    gated_hi(st, 1)
                gate_tanh(st, 1)
                if not last:
                    slot_exp(st + 1, npar)
                if first:
                    x_hi(2)
                if not last:
                    copy_v(st + 1, npar, 0)
                    copy_v(st + 1, npar, 1)
                if first:
                    inner_copy(2, rg[1])
                if bp == 3 and more:
                    split_hi(hp + 1, W_QK)
                    prepare_scales(hp + 1)
                    prepare_out(hp + 1)
                act.wait_ge(sub_done, st + 1)
                act.activation(sm[:, :], sm[:, :], ACT.Exp).then_inc(p_ready, 1)
                if not last:
                    copy_v(st + 1, npar, 2)
                    copy_v(st + 1, npar, 3)
                hidden_hi(st, 0)
                hidden_hi(st, 1)
                if not last:
                    swap_halves(st + 1, 0)
                    swap_halves(st + 1, 1)
                for i in range(4):
                    if first and i == 2:
                        x_hi(3)
                    if not last and i > 1:
                        swap_halves(st + 1, i)
                    off_diagonal(*w_args, i, 1.0)
                    if i == 1 and bp == 3 and more:
                        split_hi(hp + 1, W_GU)
                    if i == 1 and bp == 2 and more:
                        split_slot(hp + 1)
                if first:
                    inner_copy(3, rg[1])
                square_o(st, 0)
                if not last:
                    copy_J(st + 1, 0, sc_bank(bp, "E", 0)[:, :])
                    copy_J(st + 1, 1, sc_bank(bp, "E", 1)[:, :])
                square_o(st, 1)

            each_stage(act, stage)
            gated_hi(STEPS, 0)
            gated_hi(STEPS, 1)

        @block.vector
        def _(dve):
            cos = rope[:, 0, :].unsqueeze(1).to_broadcast([P, 2, T])
            sin = rope[:, 1, :].unsqueeze(1).to_broadcast([P, 2, T])

            def two(ap):
                return ap.rearrange("p (b t) -> p b t", b=2)

            def diagonal(full, done, dst, bp, kind, st, i, mask, used):
                dve.wait_ge(full, 4 * st + i + 1)
                wait(dve, *used)
                src = sc_bank(bp, kind, i)[:, 0:3 * P].rearrange("p (n t) -> p n t", n=3)
                dve.tensor_tensor(dst[i][:, 0:3:2, :], src[:, 0:3:2, :], mask[:, :, :], ALU.mult).then_inc(done, 1)

            def sum_squares(st, b):
                dve.wait_ge(osq_done, 2 * st + b + 1)
                wait(dve, msn_done, st)
                dve.tensor_reduce(ms[:, 4 * b:4 * b + 4], osq[:, :].rearrange("p (g d) -> p g d", g=4),
                                  AX_X, ALU.add).then_inc(ms_done, 1)

            def norm_arg(done):
                dve.wait_ge(ms_done, 2 * done)
                dve.wait_ge(rs2_done, done)
                wait(dve, mse_done, done - 1)
                dve.tensor_tensor(msn[:, :], ms[:, :], rs2[:, :], ALU.mult).then_inc(msn_done, 1)
                dve.wait_ge(msn_done, done)
                wait(dve, pow_done, done - 1)
                dve.tensor_scalar(mse[:, :], msn[:, :], 1.0 / DV, EPS, ALU.mult, ALU.add).then_inc(mse_done, 1)

            def gate_scale(done):
                dve.wait_ge(pow_done, done)
                wait(dve, og_done, 2 * (done - 1))
                dve.tensor_tensor(scal[:, :], rstd[:, :], rs[:, :], ALU.mult).then_inc(scal_done, 1)
                dve.wait_ge(scal_done, done)
                wait(dve, ogT_full, 2 * (done - 1))

            def gate_o(par, b):
                for q in range(4):
                    c = slice((4 * b + q) * P, (4 * b + q + 1) * P)
                    ins = dve.scalar_tensor_tensor(
                        out=og[:, c], in0=rg[b][:, q * P:(q + 1) * P], scalar=scal[:, 4 * b + q:4 * b + q + 1],
                        in1=G[par][:, c], op0=ALU.mult, op1=ALU.mult)
                ins.then_inc(og_done, 1)

            def gated_lo(done, h):
                dve.wait_ge(ogT_hi, 2 * (done - 1) + h + 1)
                wait(dve, out_full, 2 * (done - 1))
                dve.tensor_tensor(ogT[1][h][:, :], rg[h][:, :], ogT[0][h][:, :].bitcast(F32),
                                  ALU.subtract).then_inc(ogT_lo, 1)

            def clip(n, par, src):
                dve.wait_ge(S_full, n + 1)
                wait(dve, W_full, 4 * (n - 1))
                wait(dve, scan_done, 2 * (n - 1))
                dve.tensor_scalar(esT[par][:, :], src, CLAMP, -CLAMP, ALU.min, ALU.max).then_inc(clip_done, 1)

            def gate_g(n, par, i):
                dve.wait_ge(gtanh, 4 * n + i + 1)
                if i == 0:
                    wait(dve, og_done, 2 * (n - 1))
                dve.scalar_tensor_tensor(out=G[par][:, i * 256:(i + 1) * 256], in0=th[i % 2][:, :], scalar=1.0,
                                         in1=pj[i][:, 256:512], op0=ALU.add, op1=ALU.mult).then_inc(G_ready, 1)

            def cumulate(n, par):
                dve.wait_ge(es_ready, n + 1)
                wait(dve, E_full, 2 * (n - 1))
                wait(dve, qe_ready, n - 1)
                for b in range(2):
                    c = slice(b * T, (b + 1) * T)
                    dve.tensor_tensor_scan(enzT[par][:, c], esT[par][:, c], esT[par][:, c], 0.0,
                                           ALU.add, ALU.max).then_inc(scan_done, 1)

            def invert(n, par, b):
                dve.wait_ge(scan_done, 2 * n + b + 1)
                c = slice(b * T, (b + 1) * T)
                dve.reciprocal(enzT[par][:, c], enzT[par][:, c]).then_inc(enz_ready, 1)

            def softmax_in(st):
                dve.wait_ge(ok_full, st + 1)
                dve.wait_ge(J_ready, 2 * st + 2)
                wait(dve, pT_full, st)
                wait(dve, ssum_done, st)
                dve.tensor_tensor(sm[:, :], rg[0][:, :], enzJ[:, :], ALU.mult).then_inc(okz_done, 1)
                dve.wait_ge(okz_done, st + 1)
                dve.tensor_reduce(mx[:, :], sm[:, :].rearrange("p (g m) -> p g m", m=M),
                                  AX_X, ALU.max).then_inc(mx_done, 1)

            def softmax_sum(st):
                dve.wait_ge(p_ready, st + 1)
                wait(dve, rs_done, st)
                dve.tensor_reduce(ssum[:, :], sm[:, :].rearrange("p (g m) -> p g m", m=M),
                                  AX_X, ALU.add).then_inc(ssum_done, 1)

            def softmax_inverse(st):
                dve.wait_ge(ssum_done, st + 1)
                wait(dve, scal_done, st)
                dve.reciprocal(rs[:, :], ssum[:, :]).then_inc(rs_done, 1)
                dve.wait_ge(rs_done, st + 1)
                wait(dve, msn_done, st)
                dve.tensor_tensor(rs2[:, :], rs[:, :], rs[:, :], ALU.mult).then_inc(rs2_done, 1)

            def add_share(done, bp, b):
                dve.wait_ge(out_full, 2 * (done - 1) + b + 1)
                wait(dve, acc_done, 2 * (done - 1) + b)
                a = acc[:, bp * NT + 2 * b:bp * NT + 2 * b + 2, :].rearrange("p n c -> p (n c)")
                dve.tensor_tensor(a, rg[1 - b][:, :], a, ALU.add).then_inc(acc_done, 1)

            def gate_arg(st, e):
                dve.wait_ge(ff_sq, 2 * st + e + 1)
                wait(dve, inter_lo, 2 * (st - 1) + e + 1)
                dve.scalar_tensor_tensor(out=ffb[e][:, :], in0=ffa[e][:, :], scalar=1.0, in1=pj[2 * e][:, :],
                                         op0=ALU.add, op1=ALU.mult).then_inc(ff_arg, 1)

            def gate_gelu(st, e):
                dve.wait_ge(ff_tanh, 2 * st + e + 1)
                dve.scalar_tensor_tensor(out=ffa[e][:, :], in0=ffb[e][:, :], scalar=1.0, in1=pj[2 * e][:, :],
                                         op0=ALU.add, op1=ALU.mult).then_inc(ff_gelu, 1)

            def hidden(st, e):
                dve.wait_ge(ff_gelu, 2 * st + e + 1)
                dve.wait_ge(ffn_full, 4 * st + 2 * e + 2)
                dve.tensor_tensor(ffb[e][:, :], pj[2 * e + 1][:, :], ffa[e][:, :], ALU.mult).then_inc(inter_done, 1)

            def slot_query(st, par):
                dve.wait_ge(pT_full, st + 1)
                wait(dve, W_full, 4 * st)
                dve.tensor_tensor(qe[:, :], rg[1][:, :], enzT[par][:, :], ALU.mult).then_inc(qe_ready, 1)

            def rope_cos(n, i):
                dve.wait_ge(swapped, 4 * n + i + 1)
                wait(dve, roped, 4 * n + i - 1)
                dve.tensor_tensor(two(ra[i % 2][:, :]), two(pj[i][:, :]), cos, ALU.mult).then_inc(cos_done, 1)

            def rope_sin(n, i):
                dve.tensor_tensor(two(xs[i % 2][:, :]), two(xs[i % 2][:, :]), sin, ALU.mult).then_inc(sin_done, 1)

            def decode(hp, part):
                if part == 0:
                    dve.wait_ge(packed_in, 16 * hp + 16)
                    ins = dve.tensor_scalar(packed[:, :], packed[:, :], 0xFF, None, ALU.bitwise_and)
                else:
                    dve.wait_ge(code_step, 5 * hp + part)
                if part == 1:
                    ins = dve.scalar_tensor_tensor(out=codes[:, :], in0=packed[:, :], scalar=12, in1=packed[:, :],
                                                   op0=ALU.logical_shift_left, op1=ALU.bitwise_or)
                if part == 2:
                    ins = dve.tensor_scalar(packed[:, :], codes[:, :], 9, 0x0E000E00, ALU.logical_shift_left,
                                            ALU.bitwise_and)
                if part == 3:
                    ins = dve.tensor_scalar(codes[:, :], codes[:, :], 12, -0x7FFF8000, ALU.logical_shift_left,
                                            ALU.bitwise_and)
                if part == 4:
                    ins = dve.tensor_tensor(packed[:, :], packed[:, :], codes[:, :], ALU.bitwise_or)
                ins.then_inc(code_step, 1)

            def normalise(bp):
                dve.wait_ge(x_in[bp], 16)
                wait(dve, mv_done, NT * bp)
                wait(dve, xn_done, bp)
                for i in range(NT):
                    dve.bn_stats(bns[:, i, :], acc[:, bp * NT + i, :]).then_inc(bn_done, 1)
                for i in range(NT):
                    dve.wait_ge(bn_done, bp * NT + i + 1)
                    if i == 0 and bp:
                        dve.wait_ge(xpow_done, bp)
                    dve.bn_aggr(mv[:, i, :], bns[:, i, :]).then_inc(mv_done, 1)
                dve.wait_ge(mv_done, (bp + 1) * NT)
                dve.tensor_scalar(mse[:, 0:NT], mv[:, :, 1], EPS, None, ALU.add).then_inc(var_done, 1)
                dve.wait_ge(xpow_done, bp + 1)
                for i in range(NT):
                    ins = dve.tensor_scalar(xn[bp][:, i, :], acc[:, bp * NT + i, :], mv[:, i, 0:1],
                                            rstd[:, i:i + 1], ALU.subtract, ALU.mult)
                ins.then_inc(xn_done, 1)

            def x_lo(bp):
                for k in range(KT):
                    dve.wait_ge(xh_done, KT * bp + k + 1)
                    dve.tensor_tensor(xl[:, k, tokens(bp)], rg[k][:, :], xh[:, k, tokens(bp)].bitcast(F32),
                                      ALU.subtract).then_inc(xl_done, 1)

            def slot_lo(hp):
                rows = slice(GROUP, 2 * GROUP)
                dve.wait_ge(ws2_hi, hp + 1)
                dve.tensor_tensor(ws2[rows, :], ws2_raw[rows, :], ws2[rows, :].bitcast(F32),
                                   ALU.subtract).then_inc(ws2_lo, 4)

            def inner_lo(bp, src):
                dve.wait_ge(h1_done, 2 * bp + 2)
                dve.tensor_tensor(h1[2 * GROUP:2 * GROUP + RANK, bp, :], src[0:RANK, :],
                                  h1[0:RANK, bp, :].bitcast(F32), ALU.subtract).then_inc(h1_lo, 1)

            normalise(0)
            x_lo(0)
            normalise(1)
            slot_lo(0)
            inner_lo(0, sc[0])
            gate_g(0, 0, 0)
            decode(0, 0)
            gate_g(0, 0, 1)
            decode(0, 1)
            gate_g(0, 0, 2)
            clip(0, 0, sc[1][:, :])
            decode(0, 2)
            gate_g(0, 0, 3)
            decode(0, 3)
            decode(0, 4)
            x_lo(1)
            cumulate(0, 0)
            dve.wait_ge(const_in, 32)
            for i in range(4):
                rope_cos(0, i)
                rope_sin(0, i)
                if i == 2:
                    inner_lo(1, rg[0])

            def stage(hp, bp, first, last):
                st = 4 * hp + bp
                par, npar, pbp = bp % 2, (bp + 1) % 2, (bp - 1) % BP
                more = not (isinstance(hp, int) and hp == HP - 1)
                a_args = (A_full, A_diag, At, bp, "A", st)
                w_args = (W_full, W_diag, Wt, bp, "W", st)
                if bp == 3 and more:
                    slot_lo(hp + 1)
                diagonal(*a_args, 0, mask_a, (ok_full, st))
                if not first:
                    sum_squares(st - 1, 1)
                diagonal(*a_args, 1, mask_a, (ok_full, st))
                if first:
                    invert(0, 0, 0)
                else:
                    norm_arg(st)
                gate_arg(st, 0)
                if first:
                    invert(0, 0, 1)
                if not first:
                    gate_scale(st)
                    gate_o(npar, 0)
                diagonal(*a_args, 2, mask_a, (ok_full, st))
                if not first:
                    gate_o(npar, 1)
                gate_gelu(st, 0)
                diagonal(*a_args, 3, mask_a, (ok_full, st))
                hidden(st, 0)
                if first:
                    normalise(2)
                gate_arg(st, 1)
                if not first:
                    gated_lo(st, 0)
                if not last:
                    clip(st + 1, npar, sc_bank(bp, "S")[:, :])
                if not first:
                    gated_lo(st, 1)
                gate_gelu(st, 1)
                hidden(st, 1)
                if first:
                    x_lo(2)
                if not last:
                    gate_g(st + 1, npar, 0)
                    cumulate(st + 1, npar)
                    gate_g(st + 1, npar, 1)
                if first:
                    inner_lo(2, rg[1])
                softmax_in(st)
                if not last:
                    invert(st + 1, npar, 0)
                if not first:
                    add_share(st, pbp, 0)
                if bp == 2 and more:
                    decode(hp + 1, 2)
                if bp == 3 and more:
                    decode(hp + 1, 4)
                if not last:
                    invert(st + 1, npar, 1)
                    gate_g(st + 1, npar, 2)
                softmax_sum(st)
                softmax_inverse(st)
                if not first:
                    add_share(st, pbp, 1)
                if not last:
                    gate_g(st + 1, npar, 3)
                slot_query(st, par)
                if first:
                    normalise(3)
                if bp == 1 and more:
                    decode(hp + 1, 0)
                if not last:
                    rope_cos(st + 1, 0)
                    rope_sin(st + 1, 0)
                for i in range(4):
                    if first and i == 2:
                        x_lo(3)
                    diagonal(*w_args, i, mask_w, (o_full, 2 * st))
                    if not last and i:
                        rope_cos(st + 1, i)
                        rope_sin(st + 1, i)
                if first:
                    inner_lo(3, rg[1])
                sum_squares(st, 0)
                if bp == 1 and more:
                    decode(hp + 1, 1)
                if bp == 2 and more:
                    decode(hp + 1, 3)

            each_stage(dve, stage)
            sum_squares(STEPS - 1, 1)
            norm_arg(STEPS)
            gate_scale(STEPS)
            gate_o((BP - 1) % 2, 0)
            gate_o((BP - 1) % 2, 1)
            gated_lo(STEPS, 0)
            gated_lo(STEPS, 1)
            add_share(STEPS, BP - 1, 0)
            add_share(STEPS, BP - 1, 1)

        @block.gpsimd
        def _(pool):
            def split_lo(hp, which):
                pool.wait_ge(w_hi, 4 * hp + which + 1)
                if which == W_VG:
                    dst, src, hi = wvg[1][:, :, :], raw_k[:, :, 512:1024], wvg[0][:, :, :]
                elif which == W_QK:
                    dst, src, hi = wqk[1][:, :, :], raw_k[:, :, 0:512], wqk[0][:, :, :]
                elif which == W_GU:
                    dst, src, hi = wgu[1][:, :, :], mlp_raw, wgu[0][:, :, :]
                else:
                    dst, src, hi = (wod[1][:, :, :].rearrange("p s c -> p (s c)"), od_raw,
                                    wod[0][:, :, :].rearrange("p s c -> p (s c)"))
                pool.tensor_tensor(dst, src, hi.bitcast(F32), ALU.subtract).then_inc(w_lo, 1)

            def dequantise(hp, which):
                halves = packed[:, :].bitcast(F16).rearrange("p (n two) -> p n two", two=2)
                pool.wait_ge(code_step, 5 * hp + 5)
                pool.wait_ge(scales_set, hp + 1)
                if which == W_GU:
                    pool.wait_ge(w_lo, 4 * hp + W_QK + 1)
                    for k in range(KT):
                        pool.tensor_tensor(mlp_raw[:, k, :], halves[:, 0:512, k], scaled[:, 0:512],
                                           ALU.mult).then_inc(mlp_w, 1)
                else:
                    for e in range(2):
                        pool.tensor_tensor(od_raw[:, 512 + e * D:512 + (e + 1) * D], halves[:, 512:768, e],
                                           scaled[:, 512:768], ALU.mult).then_inc(down_w, 1)

            def rotate(n, i):
                pool.wait_ge(cos_done, 4 * n + i + 1)
                pool.wait_ge(sin_done, 4 * n + i + 1)
                wait(pool, A_full, 4 * n)
                pool.tensor_tensor(qkT[:, i, :], ra[i % 2][:, :], xs[i % 2][:, :], ALU.add).then_inc(roped, 1)

            def norm_pow(done):
                pool.wait_ge(mse_done, done)
                wait(pool, scal_done, done - 1)
                pool.tensor_tensor(rstd[:, :], mse[:, :], mhalf[:, :], ALU.pow).then_inc(pow_done, 1)

            def subtract_max(st):
                pool.wait_ge(mx_done, st + 1)
                s = sm[:, :].rearrange("p (g m) -> p g m", m=M)
                pool.tensor_tensor(s, s, mx[:, :].unsqueeze(2).to_broadcast([P, 8, M]),
                                   ALU.subtract).then_inc(sub_done, 1)

            def hidden_lo(st, e):
                pool.wait_ge(inter_hi, 2 * st + e + 1)
                pool.tensor_tensor(inter[1][e][:, :], ffb[e][:, :], inter[0][e][:, :].bitcast(F32),
                                   ALU.subtract).then_inc(inter_lo, 1)

            pool.memset(mhalf[:, :], -0.5)
            pool.memset(ident[:, :], 0.0)
            pool.memset(mask_a[:, :, :], SCALE).then_inc(const_set, 1)
            pool.memset(mask_w[:, :, :], 1.0).then_inc(const_set, 1)
            pool.memset(h1[0:2 * GROUP, :, :].bitcast(F32), 1.0).then_inc(const_set, 1)
            pool.wait_ge(const_set, 3)
            pool.memset(h1[2 * GROUP:, :, :].bitcast(F32), 0.0).then_inc(const_set, 1)
            pool.wait_ge(const_set, 4)
            pool.affine_select(out=ident[:, :], in_=ident[:, :], compare_op=ALU.not_equal, fill=1.0, base=0,
                               pattern=[[-1, P]], channel_multiplier=1)
            for m in (mask_a, mask_w):
                ins = pool.affine_select(out=m[:, :, :], in_=m[:, :, :], compare_op=ALU.is_ge, fill=0.0, base=0,
                                         pattern=[[0, 2], [1, P]], channel_multiplier=-1)
            ins.then_inc(consts, 1)

            def x_pow(bp):
                pool.wait_ge(var_done, bp + 1)
                if bp:
                    pool.wait_ge(xn_done, bp)
                pool.tensor_tensor(rstd[:, 0:NT], mse[:, 0:NT], mhalf[:, 0:NT], ALU.pow).then_inc(xpow_done, 1)

            x_pow(0)
            pool.wait_ge(ws1_hi, 1)
            pool.tensor_tensor(ws1_s[1], ws1, ws1_s[0].bitcast(F32), ALU.subtract).then_inc(ws1_lo, 1)
            split_lo(0, W_VG)
            x_pow(1)
            split_lo(0, W_QK)
            dequantise(0, W_GU)
            rotate(0, 0)
            rotate(0, 1)
            split_lo(0, W_GU)
            rotate(0, 2)
            rotate(0, 3)

            def stage(hp, bp, first, last):
                st = 4 * hp + bp
                more = not (isinstance(hp, int) and hp == HP - 1)
                if first:
                    x_pow(2)
                else:
                    norm_pow(st)
                if bp == 1:
                    dequantise(hp, W_OD)
                    split_lo(hp, W_OD)
                if bp == 3 and more:
                    split_lo(hp + 1, W_VG)
                    split_lo(hp + 1, W_QK)
                subtract_max(st)
                if first:
                    x_pow(3)
                if bp == 3 and more:
                    dequantise(hp + 1, W_GU)
                hidden_lo(st, 0)
                hidden_lo(st, 1)
                if not last:
                    for i in range(4):
                        rotate(st + 1, i)
                        if i == 1 and bp == 3 and more:
                            split_lo(hp + 1, W_GU)

            each_stage(pool, stage)
            norm_pow(STEPS)


def lay_out(a):
    c = np.ascontiguousarray

    def heads(w):
        return w.reshape(HP, 2, P, P, KT).transpose(0, 3, 4, 1, 2)

    q, k, v, g = (heads(a[f"L0_attn_{n}"]) for n in ("Wq", "Wk", "Wv", "Wg"))
    qk = np.stack([q, k], axis=4).reshape(HP, P, KT, 512)
    vg = np.stack([v, g], axis=3).reshape(HP, P, KT, 512)
    qkvg = np.concatenate([qk, vg], axis=3).reshape(HP, P, KT * 1024)

    def units(w):
        return w.reshape(HP, P, 2, w.shape[1]).transpose(0, 3, 2, 1).reshape(HP, w.shape[1], 2 * P)

    down = a["L0_ffn_down_W_packed"].reshape(D, HP, P).transpose(1, 2, 0)
    packed = np.concatenate([units(a["L0_ffn_gate_W_packed"]), units(a["L0_ffn_up_W_packed"]), down], axis=2)
    rep = P // (D // 32)
    gs, us = (np.repeat(units(a[f"L0_ffn_{n}_scales"]), rep, axis=1) for n in ("gate", "up"))
    ds = np.repeat(a["L0_ffn_down_scales"].reshape(D, HP, 8).transpose(1, 2, 0), rep, axis=1)
    wo = a["L0_attn_Wo"].reshape(D, HP, 2, P).transpose(1, 3, 2, 0).reshape(HP, P, 2 * D)
    scaled = np.concatenate([gs, us, ds, wo], axis=2)
    slot = np.zeros((HP, SLOT_K, P), a["L0_attn_Ws2"].dtype)
    slot1 = np.zeros((P, KT, P), a["L0_attn_Ws1"].dtype)
    for g in range(0, SLOT_K, GROUP):
        slot[:, g:g + RANK] = a["L0_attn_Ws2"].reshape(HP, P, RANK).transpose(0, 2, 1)
        slot[:, g + RANK] = a["L0_attn_bs2"].reshape(HP, P)
        slot1[:, :, g:g + RANK] = a["L0_attn_Ws1"].reshape(RANK, P, KT).transpose(1, 2, 0)
    return {"x": c(a["L0_attn_hidden_states"]), "w_qkvg": c(qkvg), "w_packed": c(packed), "w_scaled": c(scaled),
            "w_slot": c(slot), "w_slot1": slot1, "g_norm": c(a["L0_attn_g_norm_weight"].reshape(P, 1))}


def rope_table():
    pos = np.arange(T, dtype=np.float32)
    inv = (1.0 / np.power(np.float32(10000.0), np.arange(0, DK, 2, dtype=np.float32) / np.float32(DK))).astype(np.float32)
    ang = inv[:, None] * pos[None, :]
    cos, sin = np.cos(ang).astype(np.float32), np.sin(ang).astype(np.float32)
    return np.ascontiguousarray(np.stack([np.concatenate([cos, cos]), np.concatenate([-sin, sin])], axis=1))


def kernel(**inputs):
    import concourse.bacc as _bacc
    from concourse.bass_utils import run_bass_kernel_spmd as _run

    nc = _bacc.Bacc("TRN2", target_bir_lowering=False, num_devices=1)
    arrays = lay_out({n: np.asarray(a) for n, a in inputs.items()})
    arrays["rope_tab"] = rope_table()
    args = [nc.dram_tensor(f"in_{n}", a.shape, mybir.dt.from_np(a.dtype), kind="ExternalInput").ap()
            for n, a in arrays.items()]
    out = nc.dram_tensor("out_0", (B, T, D), F32, kind="ExternalOutput").ap()
    build(nc, *args, out)
    r = _run(nc, [{f"in_{n}": a for n, a in arrays.items()}], core_ids=[0])
    return r.results[0]["out_0"]
```
